# Optimizing a Trainium2 kernel written in Bass

```python
import numpy as np
import jax
import jax.numpy as jnp

def _softmax(x, axis=-1):
    return jax.nn.softmax(x, axis=axis)

def _gelu(x):
    return jax.nn.gelu(x, approximate=True)

def _silu(x):
    return jax.nn.silu(x)

def _sigmoid(x):
    return jax.nn.sigmoid(x)

def _layernorm(x, axis=-1, eps=1e-05):
    m = jnp.mean(x, axis=axis, keepdims=True)
    v = jnp.var(x, axis=axis, keepdims=True)
    return (x - m) / jnp.sqrt(v + eps)

def _scatter_add(tgt, idx, src, axis=0):
    return tgt.at[idx].add(src)

def _segment_sum(src, seg, n):
    return jax.ops.segment_sum(src, seg, n)
kernel_name = 'mk_xattn_ffn_d1_seqx_r4_cf50e4'

def setup_inputs(seed: int=0):
    np.random.seed(seed)
    _w = jnp.asarray

    def _rec_inputs():
        import jax
        import jax.numpy as jnp
        _rk = jax.random.key(seed)
        x = 7.22e-05 + 1 * jax.random.normal(jax.random.fold_in(_rk, 1), (2, 1024, 256), jnp.float32)
        _lenS = 1024 - jax.random.randint(jax.random.fold_in(_rk, 7), (2,), 0, max(1, 1024 // 4) + 1, jnp.int32)
        _lenS2 = 77 - jax.random.randint(jax.random.fold_in(_rk, 8), (2,), 0, max(1, 77 // 4) + 1, jnp.int32)
        _ctx_1024P = jax.random.normal(jax.random.fold_in(_rk, 11), (2, 16, 256), jnp.float32)
        _ctx_1024c = jax.random.dirichlet(jax.random.fold_in(_rk, 511), 0.3 * jnp.ones((16,), jnp.float32), (2, 77))
        _ctx_1024t = jnp.einsum('bsk,bkd->bsd', _ctx_1024c, _ctx_1024P)
        _ctx_1024t = _ctx_1024t * jax.lax.rsqrt(jnp.mean(jnp.square(_ctx_1024t)) + 1e-12) * 0.953939
        ctx_1024 = 4.13588e-05 + 0.999923 * (_ctx_1024t + 0.3 * jax.random.normal(jax.random.fold_in(_rk, 611), (2, 77, 256), jnp.float32))
        _validS = jnp.arange(1024)[None, :] < _lenS[:, None]
        _validS2 = jnp.arange(77)[None, :] < _lenS2[:, None]
        _causal = jnp.tril(jnp.ones((1024, 1024), dtype=bool))
        mask_1xSxS2_ff0 = jnp.where(jnp.ones((1, 1024, 77), dtype=bool), 0.0, -1000000000.0).astype(jnp.float32)
        return (x, ctx_1024, mask_1xSxS2_ff0)
    x, ctx_1024, mask_1xSxS2_ff0 = _rec_inputs()

    def _L0_xattn_setup():
        import jax, jax.numpy as jnp
        import numpy as np
        INP_SIZE = 256
        D_MODEL = 256
        B, S = (4, 512)
        key = jax.random.key(seed)
        ks = jax.random.split(key, 9)
        q = jax.random.normal(ks[0], (B, S, INP_SIZE), dtype=jnp.float32)
        k = jax.random.normal(ks[1], (B, S, INP_SIZE), dtype=jnp.float32)
        v = jax.random.normal(ks[2], (B, S, INP_SIZE), dtype=jnp.float32)
        mask = jnp.zeros((1, S, S), dtype=jnp.float32)
        kernel_q = jax.random.normal(ks[3], (INP_SIZE, D_MODEL), dtype=jnp.float32) * 0.05
        kernel_k = jax.random.normal(ks[4], (INP_SIZE, D_MODEL), dtype=jnp.float32) * 0.05
        kernel_v = jax.random.normal(ks[5], (INP_SIZE, D_MODEL), dtype=jnp.float32) * 0.05
        bias_q = jax.random.normal(ks[6], (D_MODEL,), dtype=jnp.float32) * 0.05
        bias_k = jax.random.normal(ks[7], (D_MODEL,), dtype=jnp.float32) * 0.05
        bias_v = jax.random.normal(ks[8], (D_MODEL,), dtype=jnp.float32) * 0.05
        return {'q': q, 'k': k, 'v': v, 'mask': mask, 'kernel_q': kernel_q, 'bias_q': bias_q, 'kernel_k': kernel_k, 'bias_k': bias_k, 'kernel_v': kernel_v, 'bias_v': bias_v}
    _L0_xattn_all = _L0_xattn_setup()
    _L0_xattn_in = {k: v for k, v in _L0_xattn_all.items() if k in ('kernel_q', 'bias_q', 'kernel_k', 'bias_k', 'kernel_v', 'bias_v')}
    del _L0_xattn_all

    def _L0_ffn_setup():
        import jax, jax.numpy as jnp
        import numpy as np
        H = 256
        I = 512
        E = 32
        B, S = (4, 512)

        def _grouped_mm(a, w, group_sizes):
            return jax.lax.ragged_dot(a, w, group_sizes)

        def _swiglu(x, gw, uw, dw):
            return jax.nn.silu(x @ gw) * (x @ uw) @ dw
        key = jax.random.key(seed)
        ks = jax.random.split(key, 8)
        scale = 0.02
        inp = {'hidden_states': jax.random.normal(ks[0], (B, S, H), dtype=jnp.float32), 'gate_w': jax.random.normal(ks[1], (H, E), dtype=jnp.float32) * scale, 'shared_gate_w': jax.random.normal(ks[2], (H, I), dtype=jnp.float32) * scale, 'shared_up_w': jax.random.normal(ks[3], (H, I), dtype=jnp.float32) * scale, 'shared_down_w': jax.random.normal(ks[4], (I, H), dtype=jnp.float32) * scale, 'routed_gate_w': jax.random.normal(ks[5], (E, H, I), dtype=jnp.float32) * scale, 'routed_up_w': jax.random.normal(ks[6], (E, H, I), dtype=jnp.float32) * scale, 'routed_down_w': jax.random.normal(ks[7], (E, I, H), dtype=jnp.float32) * scale}
        return inp
    _L0_ffn_all = _L0_ffn_setup()
    _L0_ffn_in = {k: v for k, v in _L0_ffn_all.items() if k in ('gate_w', 'shared_gate_w', 'shared_up_w', 'shared_down_w', 'routed_gate_w', 'routed_up_w', 'routed_down_w')}
    del _L0_ffn_all
    return {'x': x, 'ctx_1024': ctx_1024, 'mask_1xSxS2_ff0': mask_1xSxS2_ff0, 'L0_xattn_kernel_q': _L0_xattn_in['kernel_q'], 'L0_xattn_bias_q': _L0_xattn_in['bias_q'], 'L0_xattn_kernel_k': _L0_xattn_in['kernel_k'], 'L0_xattn_bias_k': _L0_xattn_in['bias_k'], 'L0_xattn_kernel_v': _L0_xattn_in['kernel_v'], 'L0_xattn_bias_v': _L0_xattn_in['bias_v'], 'L0_ffn_gate_w': _L0_ffn_in['gate_w'], 'L0_ffn_shared_gate_w': _L0_ffn_in['shared_gate_w'], 'L0_ffn_shared_up_w': _L0_ffn_in['shared_up_w'], 'L0_ffn_shared_down_w': _L0_ffn_in['shared_down_w'], 'L0_ffn_routed_gate_w': _L0_ffn_in['routed_gate_w'], 'L0_ffn_routed_up_w': _L0_ffn_in['routed_up_w'], 'L0_ffn_routed_down_w': _L0_ffn_in['routed_down_w']}

def reference(x, ctx_1024, mask_1xSxS2_ff0, L0_xattn_kernel_q, L0_xattn_bias_q, L0_xattn_kernel_k, L0_xattn_bias_k, L0_xattn_kernel_v, L0_xattn_bias_v, L0_ffn_gate_w, L0_ffn_shared_gate_w, L0_ffn_shared_up_w, L0_ffn_shared_down_w, L0_ffn_routed_gate_w, L0_ffn_routed_up_w, L0_ffn_routed_down_w):
    import jax
    import jax.numpy as jnp

    def _L0_xattn_ref(q, k, v, mask, kernel_q, bias_q, kernel_k, bias_k, kernel_v, bias_v):
        import jax, jax.numpy as jnp
        import numpy as np
        INP_SIZE = 256
        D_MODEL = 256
        B, S = (4, 512)
        qp = jnp.einsum('bsi,id->bsd', q, kernel_q) + bias_q
        kp = jnp.einsum('bsi,id->bsd', k, kernel_k) + bias_k
        vp = jnp.einsum('bsi,id->bsd', v, kernel_v) + bias_v
        dk = jnp.asarray(kp.shape[-1], dtype=jnp.float32)
        logits = jnp.einsum('bqd,bkd->bqk', qp, kp) / jnp.sqrt(dk)
        logits = logits + mask
        attn = jax.nn.softmax(logits, axis=-1)
        out = jnp.einsum('bqk,bkd->bqd', attn, vp)
        return out

    def _L0_ffn_ref(hidden_states, gate_w, shared_gate_w, shared_up_w, shared_down_w, routed_gate_w, routed_up_w, routed_down_w):
        import jax, jax.numpy as jnp
        import numpy as np
        H = 256
        I = 512
        E = 32
        B, S = (4, 512)

        def _grouped_mm(a, w, group_sizes):
            return jax.lax.ragged_dot(a, w, group_sizes)

        def _swiglu(x, gw, uw, dw):
            return jax.nn.silu(x @ gw) * (x @ uw) @ dw
        b, s, h = hidden_states.shape
        x = hidden_states.reshape(-1, h)
        shared_out = _swiglu(x, shared_gate_w, shared_up_w, shared_down_w)
        logits = x @ gate_w
        topk_ids = jnp.argmax(logits, axis=-1)
        topk_val = jnp.max(logits, axis=-1)
        scores = jax.nn.sigmoid(topk_val)[:, None]
        xs = x * scores
        tokens_per_expert = jnp.zeros((E,), jnp.int32).at[topk_ids].add(1)
        order = jnp.argsort(topk_ids)
        sorted_x = xs[order]
        g = _grouped_mm(sorted_x, routed_gate_w, tokens_per_expert)
        u = _grouped_mm(sorted_x, routed_up_w, tokens_per_expert)
        d = _grouped_mm(jax.nn.silu(g) * u, routed_down_w, tokens_per_expert)
        inv = jnp.argsort(order)
        routed_out = d[inv]
        return (shared_out + routed_out).reshape(b, s, h)
    x = x + _L0_xattn_ref(_layernorm(x, axis=-1), ctx_1024, ctx_1024, mask_1xSxS2_ff0, L0_xattn_kernel_q, L0_xattn_bias_q, L0_xattn_kernel_k, L0_xattn_bias_k, L0_xattn_kernel_v, L0_xattn_bias_v)
    x = x + _L0_ffn_ref(_layernorm(x, axis=-1), L0_ffn_gate_w, L0_ffn_shared_gate_w, L0_ffn_shared_up_w, L0_ffn_shared_down_w, L0_ffn_routed_gate_w, L0_ffn_routed_up_w, L0_ffn_routed_down_w)
    return x

_drawn_inputs = setup_inputs


def setup_inputs(seed=0):
    import zlib

    import numpy as np

    out = dict(_drawn_inputs(seed))
    spreads = {}
    factors = {'L0_xattn_bias_q': 8.0,
     'L0_xattn_bias_k': 64.0,
     'L0_ffn_gate_w': 6.051,
     'L0_ffn_routed_gate_w': 6.013,
     'L0_ffn_routed_up_w': 5.965,
     'L0_ffn_routed_down_w': 5.961,
     'L0_ffn_shared_gate_w': 8.0,
     'L0_ffn_shared_up_w': 8.0,
     'L0_ffn_shared_down_w': 8.0}
    for name, (base, spread) in spreads.items():
        noise = np.random.default_rng([zlib.crc32(name.encode()), seed]).standard_normal(out[name].shape)
        drawn = base * np.exp(spread * noise) if base else spread * noise
        out[name] = jnp.asarray(drawn.astype(out[name].dtype))
    for name, factor in factors.items():
        out[name] = (out[name] * factor).astype(out[name].dtype)
    return out
```

```python
from contextlib import ExitStack

import concourse.bass as bass
from concourse import mybir

ALU = mybir.AluOpType
ACT = mybir.ActivationFunctionType
AX = mybir.AxisListType
F32 = mybir.dt.float32
BF16 = mybir.dt.bfloat16
I32 = mybir.dt.int32
U32 = mybir.dt.uint32
P = 128


def build_cross_attention_moe(nc, x, ctx_in, mask, wq, bq, wk, bk, wv, bv, gate_w,
                              sh_gate_w, sh_up_w, sh_down_w, ex_gate_w, ex_up_w, ex_down_w, out):
    B, S, D = x.shape
    KV = ctx_in.shape[1]
    NE = gate_w.shape[1]
    FF = sh_gate_w.shape[1]
    T = B * S
    NT = T // P
    NTB = S // P
    NU = NT // 2
    KD = D // P
    KF = FF // P
    GT = 512
    NG = T // GT
    CH = 64
    RING = 4
    REC = 260
    EPS = 1e-5
    SCALE = float(D) ** -0.5
    assert NE % RING == 0 and D == 256 and KD == 2 and GT == 4 * P and 2 * FF * 2 // P * CH // 2 <= 512

    x_t = x.rearrange("b s d -> (b s) d").rearrange("(i p) d -> p i d", p=P)
    out_rows = out.rearrange("b s d -> (b s) d")
    out_t = out_rows.rearrange("(i p) d -> p i d", p=P)
    sorted_rows = nc.dram_tensor("sorted_rows", [T, REC], F32, kind="Internal").ap()
    sorted_t = sorted_rows.rearrange("(i p) c -> p i c", p=P)

    with ExitStack() as st:
        def sb(name, shape, dt=F32):
            return st.enter_context(nc.sbuf_tensor(name, shape, dt))

        def sem(name):
            return st.enter_context(nc.semaphore(name))

        bank = [st.enter_context(nc.psum_tensor(f"bank{i}", [P, 512], F32)) for i in range(8)]

        ident = sb("ident", [P, P])
        before = sb("before", [P, P], BF16)
        ones_bf = sb("ones_bf", [P, P], BF16)
        ones_row = sb("ones_row", [1, 2 * P])
        ones_scan = sb("ones_scan", [P, NE * NT])
        iota_e = sb("iota_e", [P, NE])
        power = sb("power", [P, 2])
        wq_sb = sb("wq_sb", [P, KD, D])
        wk_sb = sb("wk_sb", [P, KD, D])
        wv_sb = sb("wv_sb", [P, KD, D])
        bq_row = sb("bq_row", [1, D])
        bk_row = sb("bk_row", [1, D])
        bv_row = sb("bv_row", [1, D])
        ctx_sb = sb("ctx_sb", [KV, B, D])
        ctxT = sb("ctxT", [P, KD, B * KV])
        wqT = sb("wqT", [P, KD, D])
        kT = sb("kT", [P, KD, B * KV])
        bq_wide = sb("bq_wide", [P, KD, P])
        v_sb = sb("v_sb", [KV, B, D])
        qk = sb("qk", [P, KD, B * KV])
        bias_k = sb("bias_k", [P, B * KV])
        mask_sb = sb("mask_sb", [P, NTB, KV])
        mask_b = sb("mask_b", [P, B, NTB, KV])
        x1 = sb("x1", [P, NT, D])
        xn = sb("xn", [P, NT, D])
        pairT = sb("pairT", [P, 2, 2, KD, P])
        probs = sb("probs", [P, NT, KV])
        pT = sb("pT", [KV, 2, 2, P])
        stats1 = sb("stats1", [P, NT, 6])
        stats2 = sb("stats2", [P, NT, 6])
        mv1 = sb("mv1", [P, NT, 2])
        mv2 = sb("mv2", [P, NT, 2])
        var1 = sb("var1", [P, NT])
        var2 = sb("var2", [P, NT])
        rstd1 = sb("rstd1", [P, NT])
        rstd2 = sb("rstd2", [P, NT])
        nmax = sb("nmax", [P, NT])
        psum_p = sb("psum_p", [P, NT])
        rsum = sb("rsum", [P, NT])
        xnT = sb("xnT", [P, KD, T + CH])
        gate_sb = sb("gate_sb", [P, KD, NE])
        top8 = sb("top8", [P, NT, 8])
        idx8 = sb("idx8", [P, NT, 8], U32)
        half_tanh = sb("half_tanh", [P, NT])
        score = sb("score", [P, NT])
        rec = sb("rec", [P, NT, REC])
        expert_f = sb("expert_f", [P, NT])
        onehot = sb("onehot", [P, NT, NE], BF16)
        tot = sb("tot", [P, NE, NT])
        first = sb("first", [P, NE, NT])
        place = sb("place", [P, NT, NE])
        pos_f = sb("pos_f", [P, NT])
        pos = sb("pos", [P, NT], I32)
        count_f = sb("count_f", [1, NE])
        count_i = sb("count_i", [1, NE], I32)
        extra_i = sb("extra_i", [1, NE], I32)
        extra_f = sb("extra_f", [1, NE])
        extra_cum = sb("extra_cum", [1, NE])
        table = sb("table", [1, NE + 1, 4], I32)
        shg = sb("shg", [P, KD, FF])
        shu = sb("shu", [P, KD, FF])
        shd = sb("shd", [P, KF, D])
        silu_s = sb("silu_s", [P, 2, GT])
        xsT = sb("xsT", [P, KD, T + CH])
        h_s = xsT[:, :, 0:KF * GT].rearrange("p g (m t) -> p g m t", m=KF)
        yT = xnT
        silu_r = sb("silu_r", [P, 3, KF, CH])
        h_r = sb("h_r", [P, 3, KF, CH])
        ring_gu = sb("ring_gu", [P, RING, 2, KD, FF])
        ring_d = sb("ring_d", [P, RING, KF, D])
        y_rows = xn

        x_in = [sem(f"x_in{g}") for g in range(4)]
        ctx_w_in = sem("ctx_w_in")
        mask_in = sem("mask_in")
        gate_in = sem("gate_in")
        shared_in = sem("shared_in")
        w_in = [sem(f"w_in{s}") for s in range(RING)]
        scattered = sem("scattered")
        sorted_in = [sem(f"sorted_in{g}") for g in range(4)]
        residual_out = sem("residual_out")
        added_out = sem("added_out")
        pool_step = sem("pool_step")
        dve_step = sem("dve_step")
        consts = sem("consts")
        prep_pe = sem("prep_pe")
        prep_act = sem("prep_act")
        prep_dve = sem("prep_dve")
        ln1_stats = sem("ln1_stats")
        xn_ready = sem("xn_ready")
        tA = sem("tA")
        pairT_ready = sem("pairT_ready")
        logits_ready = sem("logits_ready")
        s_ready = sem("s_ready")
        p_ready = sem("p_ready")
        tP = sem("tP")
        pT_ready = sem("pT_ready")
        av_ready = sem("av_ready")
        x1_ready = sem("x1_ready")
        ln2_stats = sem("ln2_stats")
        rstd2_ready = sem("rstd2_ready")
        xn2_ready = sem("xn2_ready")
        tE = sem("tE")
        xnT_ready = sem("xnT_ready")
        gate_ready = sem("gate_ready")
        top_ready = sem("top_ready")
        tanh_ready = sem("tanh_ready")
        rec_ready = sem("rec_ready")
        onehot_ready = sem("onehot_ready")
        ranks_ready = sem("ranks_ready")
        ranks_read = sem("ranks_read")
        pos_ready = sem("pos_ready")
        table_ready = sem("table_ready")
        tX = sem("tX")
        xsT_ready = sem("xsT_ready")
        sh_gu = sem("sh_gu")
        sh_silu = sem("sh_silu")
        sh_h = sem("sh_h")
        sh_down = sem("sh_down")
        residual_ready = sem("residual_ready")
        gu0_ready = sem("gu0_ready")
        silu0_ready = sem("silu0_ready")
        h0_ready = sem("h0_ready")
        down0_done = sem("down0_done")
        y0_stored = sem("y0_stored")
        guX_ready = sem("guX_ready")
        siluX_ready = sem("siluX_ready")
        hX_ready = sem("hX_ready")
        downX_done = sem("downX_done")
        yX_stored = sem("yX_stored")
        tY = sem("tY")
        y_ready_act = sem("y_ready_act")
        y_ready_dve = sem("y_ready_dve")

        PARTS = "p (t n) -> p t n"
        FREE1, FREE2, FREE_H = 1, 2, 4

        def within(col):
            return nc.s_assert_within(col, 0, T, skip_runtime_bounds_check_because="a further chunk has a token in its first column")

        block = st.enter_context(nc.Block())

        def load_expert(eng, e, s):
            eng.dma_start(ring_gu[:, s, 0], ex_gate_w[bass.ds(e, 1)].rearrange("a (k p) f -> p (a k) f", p=P)).then_inc(w_in[s], 16)
            eng.dma_start(ring_gu[:, s, 1], ex_up_w[bass.ds(e, 1)].rearrange("a (k p) f -> p (a k) f", p=P)).then_inc(w_in[s], 16)
            eng.dma_start(ring_d[:, s], ex_down_w[bass.ds(e, 1)].rearrange("a (m p) d -> p (a m) d", p=P)).then_inc(w_in[s], 16)

        @block.sync
        def _(sp):
            sp.dma_start(x1[:, 0:4], x_t[:, 0:4]).then_inc(x_in[0], 16)
            sp.dma_start(ctx_sb[:], ctx_in.rearrange("b k d -> k b d")).then_inc(ctx_w_in, 16)
            for dst, src in ((wk_sb, wk), (wq_sb, wq), (wv_sb, wv)):
                sp.dma_start(dst[:], src.rearrange("(k p) d -> p k d", p=P)).then_inc(ctx_w_in, 16)
            for dst, src in ((bq_row, bq), (bk_row, bk), (bv_row, bv)):
                sp.dma_start(dst[:], src.rearrange("(a d) -> a d", a=1)).then_inc(ctx_w_in, 16)
            sp.dma_start(mask_sb[:], mask[0].rearrange("(i p) k -> p i k", p=P)).then_inc(mask_in, 16)
            for g in range(1, 4):
                sp.dma_start(x1[:, 4 * g:4 * g + 4], x_t[:, 4 * g:4 * g + 4]).then_inc(x_in[g], 16)
            sp.dma_start(gate_sb[:], gate_w.rearrange("(k p) e -> p k e", p=P)).then_inc(gate_in, 16)
            sp.dma_start(shg[:], sh_gate_w.rearrange("(k p) f -> p k f", p=P)).then_inc(shared_in, 16)
            sp.dma_start(shu[:], sh_up_w.rearrange("(k p) f -> p k f", p=P)).then_inc(shared_in, 16)
            sp.dma_start(shd[:], sh_down_w.rearrange("(m p) d -> p m d", p=P)).then_inc(shared_in, 16)
            for s in range(RING):
                load_expert(sp, s, s)
            sp.wait_ge(scattered, 16 * NT)
            for g in range(4):
                sp.dma_start(rec[:, 4 * g:4 * g + 4], sorted_t[:, 4 * g:4 * g + 4]).then_inc(sorted_in[g], 16)
            with sp.Fori(0, NU) as u:
                sp.wait_ge(residual_ready, u + FREE2 + 1)
                sp.dma_start(out_t[:, bass.ds(2 * u, 2)], x1[:, bass.ds(2 * u, 2)]).then_inc(residual_out, 16)
            with sp.Fori(1, NE // RING) as it:
                for s in range(RING):
                    sp.wait_ge(down0_done, RING * it + (s - RING + 1 + FREE2))
                    load_expert(sp, RING * it + s, s)

        @block.gpsimd
        def _(pool):
            steps = [0]

            def step(ins):
                steps[0] += 1
                ins.then_inc(pool_step, 1)
                pool.wait_ge(pool_step, steps[0])

            nc.gpsimd.memset(power[:], -0.5).then_inc(consts, 1)
            step(nc.gpsimd.memset(ident[:], 0.0))
            nc.gpsimd.affine_select(out=ident[:], in_=ident[:], compare_op=ALU.not_equal, fill=1.0, base=0,
                                    pattern=[[-1, P]], channel_multiplier=1).then_inc(consts, 1)
            nc.gpsimd.memset(ones_row[:], 1.0).then_inc(consts, 1)
            nc.gpsimd.memset(ones_bf[:], 1.0).then_inc(consts, 1)
            step(nc.gpsimd.memset(before[:], 0.0))
            nc.gpsimd.affine_select(out=before[:], in_=before[:], compare_op=ALU.is_ge, fill=1.0, base=0,
                                    pattern=[[-1, P]], channel_multiplier=1).then_inc(consts, 1)
            nc.gpsimd.iota(iota_e[:], pattern=[[1, NE]], base=0, channel_multiplier=0,
                           allow_small_or_imprecise_dtypes=True).then_inc(consts, 1)
            nc.gpsimd.memset(ones_scan[:], 1.0).then_inc(consts, 1)
            nc.gpsimd.memset(xsT[:, :, T:T + CH], 0.0).then_inc(consts, 1)
            step(nc.gpsimd.memset(rec[:, :, D:REC], 0.0))
            step(nc.gpsimd.iota(rec[:, :, D:D + 1].bitcast(I32), pattern=[[P, NT], [0, 1]], base=0, channel_multiplier=1))
            pool.wait_ge(consts, 1)

            def norm1(u):
                a = 2 * u
                pool.wait_ge(ln1_stats, 2 * u + 2)
                step(nc.gpsimd.tensor_scalar(var1[:, a:a + 2], mv1[:, a:a + 2, 1], EPS, None, ALU.add))
                step(nc.gpsimd.tensor_tensor(rstd1[:, a:a + 2], var1[:, a:a + 2], power[:], ALU.pow))
                for i in (a, a + 1):
                    nc.gpsimd.tensor_scalar(xn[:, i], x1[:, i], mv1[:, i, 0:1], rstd1[:, i:i + 1],
                                            ALU.subtract, ALU.mult).then_inc(xn_ready, 1)

            def rstd_2(u):
                a = 2 * u
                pool.wait_ge(ln2_stats, 2 * u + 2)
                step(nc.gpsimd.tensor_scalar(var2[:, a:a + 2], mv2[:, a:a + 2, 1], EPS, None, ALU.add))
                nc.gpsimd.tensor_tensor(rstd2[:, a:a + 2], var2[:, a:a + 2], power[:], ALU.pow).then_inc(rstd2_ready, 1)

            def scaled(u):
                a = 2 * u
                pool.wait_ge(tanh_ready, u + 1)
                step(nc.gpsimd.tensor_scalar(score[:, a:a + 2], half_tanh[:, a:a + 2], 0.5, 0.5, ALU.mult, ALU.add))
                pool.wait_ge(xn2_ready, 2 * u + 2)
                for i in (a, a + 1):
                    nc.gpsimd.tensor_scalar(rec[:, i, 0:D], xn[:, i], score[:, i:i + 1], None,
                                            ALU.mult).then_inc(rec_ready, 1)

            for t in range(NU + 4):
                if t < NU:
                    norm1(t)
                if 0 <= t - 2 < NU:
                    rstd_2(t - 2)
                if 0 <= t - 4 < NU:
                    scaled(t - 4)
            pool.wait_ge(rec_ready, NT)
            pool.wait_ge(pos_ready, 1)
            for i in range(NT):
                nc.gpsimd.indirect_dma_start(
                    out=sorted_rows, out_offset=bass.IndirectOffsetOnAxis(ap=pos[:, i:i + 1], axis=0),
                    in_=rec[:, i, :], in_offset=None).then_inc(scattered, 16)
            for g in range(4):
                pool.wait_ge(sorted_in[g], 16)
            pool.wait_ge(residual_out, 16 * NU)
            for i in range(NT):
                pool.wait_ge(y_ready_dve if i // 2 % 2 else y_ready_act, i // 4 + 1)
                nc.gpsimd.indirect_dma_start(
                    out=out_rows, out_offset=bass.IndirectOffsetOnAxis(ap=rec[:, i, D:D + 1].bitcast(I32), axis=0),
                    in_=y_rows[:, i, :], in_offset=None, compute_op=ALU.add).then_inc(added_out, 16)
            pool.wait_ge(added_out, 16 * NT)

        @block.vector
        def _(dve):
            v = nc.vector
            steps = [0]

            def step(ins):
                steps[0] += 1
                ins.then_inc(dve_step, 1)
                dve.wait_ge(dve_step, steps[0])

            def layer_stats(u, stats, mv, done):
                a = 2 * u
                steps[0] += 1
                v.bn_stats(stats[:, a], x1[:, a]).then_inc(dve_step, 1)
                step(v.bn_stats(stats[:, a + 1], x1[:, a + 1]))
                for i in (a, a + 1):
                    v.bn_aggr(mv[:, i], stats[:, i]).then_inc(done, 1)

            def stage_stats1(u):
                dve.wait_ge(x_in[u // 2], 16)
                layer_stats(u, stats1, mv1, ln1_stats)

            def stage_mask(u):
                a = 2 * u
                dve.wait_ge(logits_ready, u + 1)
                step(v.tensor_tensor(probs[:, a:a + 2], bank[1][:, 0:2 * KV].rearrange(PARTS, t=2),
                                     mask_b[:, a // NTB, a % NTB:a % NTB + 2], ALU.add))
                v.tensor_reduce(nmax[:, a:a + 2], probs[:, a:a + 2], AX.X, ALU.max, negate=True).then_inc(s_ready, 1)

            def stage_x1(u):
                a = 2 * u
                dve.wait_ge(p_ready, 2 * u + 2)
                step(v.reciprocal(rsum[:, a:a + 2], psum_p[:, a:a + 2]))
                dve.wait_ge(av_ready, u + 1)
                dve.wait_ge(xn_ready, 2 * u + 2)
                for j in (0, 1):
                    v.scalar_tensor_tensor(out=x1[:, a + j], in0=bank[3][:, j * D:(j + 1) * D],
                                           scalar=rsum[:, a + j:a + j + 1], in1=x1[:, a + j],
                                           op0=ALU.mult, op1=ALU.add).then_inc(x1_ready, 1)
                dve.wait_ge(x1_ready, 2 * u + 2)
                layer_stats(u, stats2, mv2, ln2_stats)

            def stage_xn2(u):
                a = 2 * u
                dve.wait_ge(rstd2_ready, u + 1)
                for i in (a, a + 1):
                    v.tensor_scalar(xn[:, i], x1[:, i], mv2[:, i, 0:1], rstd2[:, i:i + 1],
                                    ALU.subtract, ALU.mult).then_inc(xn2_ready, 1)

            def stage_top(u):
                a = 2 * u
                dve.wait_ge(gate_ready, u + 1)
                for j in (0, 1):
                    g = bank[5][:, j * NE:(j + 1) * NE]
                    step(v.max(top8[:, a + j], g))
                    v.max_index(idx8[:, a + j], top8[:, a + j], g).then_inc(top_ready, 1)

            dve.wait_ge(prep_pe, 1)
            v.tensor_copy(ctxT[:].rearrange("p k n -> p (k n)"), bank[6][:, 0:KD * B * KV]).then_inc(prep_dve, 1)
            dve.wait_ge(prep_pe, 4)
            v.tensor_copy(kT[:].rearrange("p k n -> p (k n)"), bank[5][:, 0:KD * B * KV]).then_inc(prep_dve, 1)
            stage_stats1(0)
            stage_stats1(1)
            dve.wait_ge(prep_pe, 6)
            step(v.tensor_scalar(bias_k[:], bank[1][:, 0:B * KV], SCALE, None, ALU.mult))
            dve.wait_ge(mask_in, 16)
            for b in range(B):
                v.tensor_tensor(mask_b[:, b], mask_sb[:],
                                bias_k[:, b * KV:(b + 1) * KV].rearrange("p (a k) -> p a k", a=1).to_broadcast([P, NTB, KV]),
                                ALU.add).then_inc(prep_dve, 1)
            dve.wait_ge(prep_dve, 4)
            for t in range(NU + 5):
                if 2 <= t < NU:
                    stage_stats1(t)
                if 0 <= t - 1 < NU:
                    stage_mask(t - 1)
                if 0 <= t - 2 < NU:
                    stage_x1(t - 2)
                if 0 <= t - 3 < NU:
                    stage_xn2(t - 3)
                if 0 <= t - 4 < NU:
                    stage_top(t - 4)

            dve.wait_ge(top_ready, NT)
            dve.wait_ge(consts, 8)
            step(v.tensor_copy(expert_f[:], idx8[:, :, 0]))
            v.tensor_tensor(onehot[:], iota_e[:].rearrange("p (a e) -> p a e", a=1).to_broadcast([P, NT, NE]),
                            expert_f[:].rearrange("p (i a) -> p i a", a=1).to_broadcast([P, NT, NE]),
                            ALU.is_equal).then_inc(onehot_ready, 1)
            dve.wait_ge(onehot_ready, 1)
            dve.wait_ge(ranks_ready, 1)
            step(v.tensor_copy(tot[:], bank[7][:].rearrange("p (i e) -> p e i", e=NE)))
            flat = "p e i -> p (e i)"
            step(v.tensor_tensor_scan(first[:].rearrange(flat), ones_scan[:], tot[:].rearrange(flat), 0.0,
                                      ALU.mult, ALU.add))
            step(v.tensor_tensor(first[:], first[:], tot[:], ALU.subtract))
            step(v.tensor_tensor(place[:], bank[6][:].rearrange("p (i e) -> p i e", e=NE),
                                 first[:].rearrange("p e i -> p i e"), ALU.add))
            step(v.tensor_tensor(place[:], place[:], onehot[:], ALU.mult))
            step(v.tensor_reduce(pos_f[:], place[:], AX.X, ALU.add))
            v.tensor_copy(pos[:], pos_f[:]).then_inc(pos_ready, 1)
            step(v.tensor_reduce(count_f[:], tot[0:1], AX.X, ALU.add))
            step(v.tensor_scalar(count_f[:], count_f[:], -1.0, 0.0, ALU.add, ALU.max))
            step(v.tensor_copy(count_i[:], count_f[:]))
            step(v.tensor_scalar(extra_i[:], count_i[:], CH.bit_length() - 1, None, ALU.arith_shift_right))
            step(v.tensor_copy(extra_f[:], extra_i[:]))
            step(v.tensor_tensor_scan(extra_cum[:], ones_scan[0:1, 0:NE], extra_f[:], 0.0, ALU.mult, ALU.add))
            step(v.memset(table[:], 0))
            v.tensor_copy(table[:, 0:NE, 0], first[0:1, :, 0]).then_inc(table_ready, 1)
            v.tensor_copy(table[:, 0:NE, 1], extra_f[:]).then_inc(table_ready, 1)
            v.tensor_copy(table[:, 1:NE + 1, 2], extra_cum[:]).then_inc(table_ready, 1)
            v.tensor_copy(table[:, 1:NE + 1, 3], first[0:1, :, 0]).then_inc(table_ready, 1)

            with dve.Fori(0, NG // 2) as it:
                def shared_h(g2, m):
                    n = KF * g2 + m
                    dve.wait_ge(sh_silu, 2 * KF * it + n + 1)
                    dve.wait_ge(sh_down, 4 * it + 2 * g2 - 4 + 2 + FREE_H)
                    v.tensor_tensor(h_s[:, g2, m], silu_s[:, n % 2], bank[2 + n % 2][:], ALU.mult).then_inc(sh_h, 1)

                def shared_residual(w):
                    dve.wait_ge(sh_down, 4 * it + w + 1 + FREE_H)
                    rows = x1[:, bass.ds(2 * (4 * it + w), 2)]
                    v.tensor_tensor(rows, bank[4 + w % 2][:].rearrange(PARTS, t=2), rows, ALU.add).then_inc(residual_ready, 1)

                for m in range(KF):
                    shared_h(0, m)
                shared_h(1, 0)
                shared_h(1, 1)
                shared_residual(0)
                shared_residual(1)
                shared_h(1, 2)
                shared_h(1, 3)
                shared_residual(2)
                shared_residual(3)

            dve.wait_ge(table_ready, 4)

            def h_chunk(silu_done, read, h_done, n, b):
                dve.wait_ge(silu_done, n + 1)
                dve.wait_ge(read, n + 1)
                v.tensor_tensor(h_r[:, b].rearrange("p m c -> p (m c)"),
                                silu_r[:, b].rearrange("p m c -> p (m c)"),
                                bank[b][:, KF * CH:2 * KF * CH], ALU.mult).then_inc(h_done, 1)

            def store(done, n, b, col, stored, earlier, n_earlier):
                dve.wait_ge(done, n)
                dve.wait_ge(earlier, n_earlier)
                v.tensor_copy(yT[:, :, bass.ds(col, CH)],
                              bank[3 + b][:, 0:KD * CH].rearrange(PARTS, t=KD)).then_inc(stored, 1)

            with dve.Fori(0, NE // RING) as it:
                for s in range(RING):
                    e = RING * it + s
                    q = s % 2
                    off = dve.value_load(table[0:1, bass.ds(e, 1), 0], min_val=0, max_val=T)
                    nx = dve.value_load(table[0:1, bass.ds(e, 1), 1], min_val=0, max_val=T // CH - 1)
                    xb = dve.value_load(table[0:1, bass.ds(e, 1), 2], min_val=0, max_val=T // CH - 1)
                    h_chunk(silu0_ready, down0_done, h0_ready, e, q)
                    with dve.If(nx > 0):
                        h_chunk(siluX_ready, downX_done, hX_ready, xb, 2)
                    prev = dve.value_load(table[0:1, bass.ds(e, 1), 3], min_val=0, max_val=T)
                    if s:
                        dve.wait_ge(yX_stored, xb + FREE1)
                        store(down0_done, e + FREE2, (s - 1) % 2, prev, y0_stored, y0_stored, e - 1 + FREE2)
                    else:
                        with dve.If(it > 0):
                            dve.wait_ge(yX_stored, xb + FREE1)
                            store(down0_done, e + FREE2, 1, prev, y0_stored, y0_stored, e - 1 + FREE2)
                    with dve.If(nx > 0):
                        store(downX_done, xb + 1 + FREE1, 2, within(off + CH), yX_stored, y0_stored, e + FREE2)
                    with dve.If(nx > 1):
                        with dve.Fori(1, nx) as c:
                            h_chunk(siluX_ready, downX_done, hX_ready, xb + c, 2)
                            store(downX_done, xb + c + 1 + FREE1, 2, within(off + CH * c + CH), yX_stored, y0_stored, e + FREE2)
                        dve.nop()
            last = dve.value_load(table[0:1, NE:NE + 1, 3], min_val=0, max_val=T)
            chunks = dve.value_load(table[0:1, NE:NE + 1, 2], min_val=0, max_val=T // CH - 1)
            dve.wait_ge(yX_stored, chunks + FREE1)
            store(down0_done, NE + FREE2, (NE - 1) % 2, last, y0_stored, y0_stored, NE - 1 + FREE2)
            for u in range(1, NU, 2):
                dve.wait_ge(tY, u + 1)
                v.tensor_copy(y_rows[:, 2 * u:2 * u + 2], bank[7][:].rearrange(PARTS, t=2)).then_inc(y_ready_dve, 1)

        @block.scalar
        def _(act):
            a_ = nc.scalar

            act.wait_ge(prep_pe, 2)
            a_.copy(wqT[:].rearrange("p k n -> p (k n)"), bank[7][:]).then_inc(prep_act, 1)
            act.wait_ge(prep_pe, 3)
            a_.copy(bq_wide[:].rearrange("p k n -> p (k n)"), bank[4][:, 0:KD * P]).then_inc(prep_act, 1)
            act.wait_ge(prep_pe, 5)
            a_.copy(v_sb[:].rearrange("p k n -> p (k n)"), bank[3][0:KV, 0:B * D]).then_inc(prep_act, 1)
            act.wait_ge(prep_pe, 7)
            a_.mul(qk[:].rearrange("p k n -> p (k n)"), bank[2][:, 0:KD * B * KV], SCALE).then_inc(prep_act, 1)

            def keep_normT(u):
                act.wait_ge(tA, u + 1)
                if u >= 2:
                    act.wait_ge(logits_ready, u - 1)
                a_.copy(pairT[:, u % 2].rearrange("p j k c -> p (j k c)"), bank[0][:]).then_inc(pairT_ready, 1)

            def exponentials(u):
                act.wait_ge(s_ready, u + 1)
                for i in (2 * u, 2 * u + 1):
                    a_.activation(probs[:, i], probs[:, i], ACT.Exp, bias=nmax[:, i:i + 1],
                                  accum_out=psum_p[:, i:i + 1]).then_inc(p_ready, 1)

            def keep_probsT(u):
                act.wait_ge(tP, u + 1)
                if u >= 2:
                    act.wait_ge(av_ready, u - 1)
                a_.copy(pT[:, u % 2].rearrange("p j c -> p (j c)"), bank[2][0:KV, 0:2 * P]).then_inc(pT_ready, 1)

            def keep_norm2T(u):
                act.wait_ge(tE, u + 1)
                a_.copy(xnT[:, :, 2 * P * u:2 * P * (u + 1)].rearrange("p k (j c) -> p j k c", j=2),
                        bank[4][:].rearrange("p (j k c) -> p j k c", j=2, k=KD)).then_inc(xnT_ready, 1)

            def top_tanh(u):
                act.wait_ge(top_ready, 2 * u + 2)
                a_.activation(half_tanh[:, 2 * u:2 * u + 2], top8[:, 2 * u:2 * u + 2, 0], ACT.Tanh,
                              scale=0.5).then_inc(tanh_ready, 1)

            for t in range(NU + 4):
                if t < NU:
                    keep_normT(t)
                if 0 <= t - 3 < NU:
                    keep_norm2T(t - 3)
                if 0 <= t - 1 < NU:
                    exponentials(t - 1)
                    keep_probsT(t - 1)
                if 0 <= t - 4 < NU:
                    top_tanh(t - 4)

            with act.Fori(0, NG // 2) as it:
                for n in range(2 * KF):
                    act.wait_ge(sh_gu, 2 * KF * it + n + 1)
                    a_.activation(silu_s[:, n % 2], bank[n % 2][:], ACT.Silu).then_inc(sh_silu, 1)

            for u in range(NU):
                act.wait_ge(tX, u + 1)
                a_.copy(xsT[:, :, 2 * P * u:2 * P * (u + 1)].rearrange("p k (j c) -> p j k c", j=2),
                        bank[6 + u % 2][:].rearrange("p (j k c) -> p j k c", j=2, k=KD)).then_inc(xsT_ready, 1)

            act.wait_ge(table_ready, 4)

            def silu_chunk(ready, n, b, done):
                act.wait_ge(ready, n + 1)
                a_.activation(silu_r[:, b].rearrange("p m c -> p (m c)"), bank[b][:, 0:KF * CH],
                              ACT.Silu).then_inc(done, 1)

            with act.Fori(0, NE // RING) as it:
                for s in range(RING):
                    e = RING * it + s
                    nx = act.value_load(table[0:1, bass.ds(e, 1), 1], min_val=0, max_val=T // CH - 1)
                    xb = act.value_load(table[0:1, bass.ds(e, 1), 2], min_val=0, max_val=T // CH - 1)
                    silu_chunk(gu0_ready, e, s % 2, silu0_ready)
                    with act.If(nx > 0):
                        silu_chunk(guX_ready, xb, 2, siluX_ready)
                    with act.If(nx > 1):
                        with act.Fori(1, nx) as c:
                            silu_chunk(guX_ready, xb + c, 2, siluX_ready)
                        act.nop()
            for u in range(0, NU, 2):
                act.wait_ge(tY, u + 1)
                a_.copy(y_rows[:, 2 * u:2 * u + 2].rearrange("p t n -> p (t n)"), bank[6][:]).then_inc(y_ready_act, 1)

        @block.tensor
        def _(pe):
            te = nc.tensor
            for s_, n in ((sh_h, FREE2), (residual_ready, FREE2), (sh_down, FREE_H), (h0_ready, FREE2),
                          (down0_done, FREE2), (y0_stored, FREE2), (hX_ready, FREE1),
                          (downX_done, FREE1), (yX_stored, FREE1)):
                pe.sem_inc(s_, n)

            pe.wait_ge(consts, 8)
            pe.wait_ge(ctx_w_in, 16 * 7)
            for k in range(KD):
                for b in range(B):
                    c = (k * B + b) * KV
                    ins = te.transpose(bank[6][:, c:c + KV], ctx_sb[:, b, k * P:(k + 1) * P], ident[0:KV, 0:KV])
            ins.then_inc(prep_pe, 1)
            for dk in range(KD):
                for ik in range(KD):
                    ins = te.transpose(bank[7][:, dk * D + ik * P:dk * D + (ik + 1) * P],
                                       wq_sb[:, ik, dk * P:(dk + 1) * P], ident[:])
            ins.then_inc(prep_pe, 1)
            for dk in range(KD):
                ins = te.matmul(bank[4][:, dk * P:(dk + 1) * P], bq_row[:, dk * P:(dk + 1) * P],
                                ones_row[:, 0:P], start=True, stop=True)
            ins.then_inc(prep_pe, 1)
            pe.wait_ge(prep_dve, 1)
            for dk in range(KD):
                o = bank[5][:, dk * B * KV:(dk + 1) * B * KV]
                for ik in range(KD):
                    te.matmul(o, wk_sb[:, ik, dk * P:(dk + 1) * P], ctxT[:, ik], start=(ik == 0), stop=False)
                ins = te.matmul(o, bk_row[:, dk * P:(dk + 1) * P], ones_row[:, 0:B * KV], start=False, stop=True)
            ins.then_inc(prep_pe, 1)
            for b in range(B):
                o = bank[3][0:KV, b * D:(b + 1) * D]
                for ik in range(KD):
                    te.matmul(o, ctxT[:, ik, b * KV:(b + 1) * KV], wv_sb[:, ik], start=(ik == 0), stop=False)
                ins = te.matmul(o, ones_row[:, 0:KV], bv_row[:], start=False, stop=True)
            ins.then_inc(prep_pe, 1)
            pe.wait_ge(prep_dve, 2)
            pe.wait_ge(prep_act, 2)
            for dk in range(KD):
                ins = te.matmul(bank[1][:, 0:B * KV], bq_wide[:, dk], kT[:, dk], start=(dk == 0), stop=(dk == KD - 1))
            ins.then_inc(prep_pe, 1)
            for ik in range(KD):
                for dk in range(KD):
                    ins = te.matmul(bank[2][:, ik * B * KV:(ik + 1) * B * KV], wqT[:, dk, ik * P:(ik + 1) * P],
                                    kT[:, dk], start=(dk == 0), stop=(dk == KD - 1))
            ins.then_inc(prep_pe, 1)

            def transpose_pair(dst, src, u, done):
                for j in (0, 1):
                    for k in range(KD):
                        c = (j * KD + k) * P
                        ins = te.transpose(dst[:, c:c + P], src[:, 2 * u + j, k * P:(k + 1) * P], ident[:])
                ins.then_inc(done, 1)

            def norm_transposes(u):
                pe.wait_ge(xn_ready, 2 * u + 2)
                if u:
                    pe.wait_ge(pairT_ready, u)
                transpose_pair(bank[0], xn, u, tA)

            def logits(u):
                pe.wait_ge(pairT_ready, u + 1)
                if u:
                    pe.wait_ge(s_ready, u)
                b = 2 * u // NTB
                for j in (0, 1):
                    for k in range(KD):
                        ins = te.matmul(bank[1][:, j * KV:(j + 1) * KV], pairT[:, u % 2, j, k],
                                        qk[:, k, b * KV:(b + 1) * KV], start=(k == 0), stop=(k == KD - 1))
                ins.then_inc(logits_ready, 1)

            def probs_transposes(u):
                pe.wait_ge(p_ready, 2 * u + 2)
                if u:
                    pe.wait_ge(pT_ready, u)
                for j in (0, 1):
                    ins = te.transpose(bank[2][0:KV, j * P:(j + 1) * P], probs[:, 2 * u + j], ident[:])
                ins.then_inc(tP, 1)

            def attend(u):
                pe.wait_ge(pT_ready, u + 1)
                if u:
                    pe.wait_ge(x1_ready, 2 * u)
                for j in (0, 1):
                    ins = te.matmul(bank[3][:, j * D:(j + 1) * D], pT[:, u % 2, j], v_sb[:, 2 * u // NTB],
                                    start=True, stop=True)
                ins.then_inc(av_ready, 1)

            def norm2_transposes(u):
                pe.wait_ge(xn2_ready, 2 * u + 2)
                if u:
                    pe.wait_ge(xnT_ready, u)
                transpose_pair(bank[4], xn, u, tE)

            def gates(u):
                pe.wait_ge(xnT_ready, u + 1)
                if u:
                    pe.wait_ge(top_ready, 2 * u)
                for j in (0, 1):
                    for k in range(KD):
                        ins = te.matmul(bank[5][:, j * NE:(j + 1) * NE], xnT[:, k, (2 * u + j) * P:(2 * u + j + 1) * P],
                                        gate_sb[:, k], start=(k == 0), stop=(k == KD - 1))
                ins.then_inc(gate_ready, 1)

            pe.wait_ge(prep_act, 4)
            pe.wait_ge(prep_dve, 4)
            pe.wait_ge(gate_in, 16)
            for t in range(NU + 3):
                if t < NU:
                    norm_transposes(t)
                if 0 <= t - 3 < NU:
                    norm2_transposes(t - 3)
                if t < NU:
                    logits(t)
                if 0 <= t - 3 < NU:
                    gates(t - 3)
                if 0 <= t - 1 < NU:
                    probs_transposes(t - 1)
                    attend(t - 1)

            pe.wait_ge(onehot_ready, 1)
            te.matmul(bank[6][:], before[:], onehot[:].rearrange("p i e -> p (i e)"), start=True, stop=True)
            te.matmul(bank[7][:], ones_bf[:], onehot[:].rearrange("p i e -> p (i e)"), start=True, stop=True).then_inc(ranks_ready, 1)

            pe.wait_ge(shared_in, 48)
            pe.wait_ge(top_ready, NT)
            with pe.Fori(0, NG // 2) as it:
                def shared_up(g2, m):
                    n = KF * g2 + m
                    pe.wait_ge(sh_h, 2 * KF * it + n - 2 + 1 + FREE2)
                    tok = bass.ds((2 * it + g2) * GT, GT)
                    for w, b in ((shg, 0), (shu, 2)):
                        for k in range(KD):
                            ins = te.matmul(bank[b + n % 2][:], w[:, k, m * P:(m + 1) * P], xnT[:, k, tok],
                                            start=(k == 0), stop=(k == KD - 1))
                    ins.then_inc(sh_gu, 1)

                def shared_down(g2):
                    pe.wait_ge(sh_h, 2 * KF * it + KF * (g2 + 1) + FREE2)
                    for w in (2 * g2, 2 * g2 + 1):
                        pe.wait_ge(residual_ready, 4 * it + w - 2 + 1 + FREE2)
                        for j in (0, 1):
                            c = (2 * (w - 2 * g2) + j) * P
                            for m in range(KF):
                                ins = te.matmul(bank[4 + w % 2][:, j * D:(j + 1) * D], h_s[:, g2, m, c:c + P],
                                                shd[:, m], start=(m == 0), stop=(m == KF - 1))
                        ins.then_inc(sh_down, 1)

                for m in range(KF):
                    shared_up(0, m)
                shared_up(1, 0)
                shared_up(1, 1)
                shared_down(0)
                shared_up(1, 2)
                shared_up(1, 3)
                shared_down(1)

            pe.wait_ge(pos_ready, 1)
            for u in range(NU):
                if u % 2 == 0:
                    pe.wait_ge(sorted_in[u // 2], 16)
                if u >= 2:
                    pe.wait_ge(xsT_ready, u - 1)
                transpose_pair(bank[6 + u % 2], rec, u, tX)

            pe.wait_ge(xsT_ready, NU)
            pe.wait_ge(table_ready, 4)
            pe.wait_ge(residual_ready, NU + FREE2)

            def up_chunk(s, b, col, h_read, n, done):
                pe.wait_ge(h_read, n)
                for w in (0, 1):
                    for m in range(KF):
                        c = (w * KF + m) * CH
                        for k in range(KD):
                            ins = te.matmul(bank[b][:, c:c + CH], ring_gu[:, s, w, k, m * P:(m + 1) * P],
                                            xsT[:, k, bass.ds(col, CH)], start=(k == 0), stop=(k == KD - 1))
                ins.then_inc(done, 1)

            def down_chunk(s, b, h_done, n, y_read, n_read, done):
                pe.wait_ge(h_done, n)
                pe.wait_ge(y_read, n_read)
                for k in range(KD):
                    for m in range(KF):
                        ins = te.matmul(bank[3 + b][:, k * CH:(k + 1) * CH], ring_d[:, s, m, k * P:(k + 1) * P],
                                        h_r[:, b, m], start=(m == 0), stop=(m == KF - 1))
                ins.then_inc(done, 1)

            with pe.Fori(0, NE // RING) as it:
                for s in range(RING):
                    e = RING * it + s
                    off = pe.value_load(table[0:1, bass.ds(e, 1), 0], min_val=0, max_val=T)
                    nx = pe.value_load(table[0:1, bass.ds(e, 1), 1], min_val=0, max_val=T // CH - 1)
                    xb = pe.value_load(table[0:1, bass.ds(e, 1), 2], min_val=0, max_val=T // CH - 1)
                    pe.wait_ge(w_in[s], 48 * it + 48)
                    up_chunk(s, s % 2, off, h0_ready, e - 2 + 1 + FREE2, gu0_ready)
                    with pe.If(nx > 0):
                        up_chunk(s, 2, within(off + CH), hX_ready, xb + FREE1, guX_ready)
                    if s:
                        down_chunk(s - 1, (s - 1) % 2, h0_ready, e + FREE2, y0_stored, e - 1 - 2 + 1 + FREE2, down0_done)
                    else:
                        with pe.If(it > 0):
                            down_chunk(RING - 1, 1, h0_ready, e + FREE2, y0_stored, e - 1 - 2 + 1 + FREE2, down0_done)
                    with pe.If(nx > 0):
                        down_chunk(s, 2, hX_ready, xb + 1 + FREE1, yX_stored, xb + FREE1, downX_done)
                    with pe.If(nx > 1):
                        with pe.Fori(1, nx) as c:
                            up_chunk(s, 2, within(off + CH * c + CH), hX_ready, xb + c + FREE1, guX_ready)
                            down_chunk(s, 2, hX_ready, xb + c + 1 + FREE1, yX_stored, xb + c + FREE1, downX_done)
                        pe.nop()
            down_chunk(RING - 1, 1, h0_ready, NE + FREE2, y0_stored, NE - 2 + FREE2, down0_done)

            pe.wait_ge(y0_stored, NE + FREE2)
            for u in range(NU):
                if u >= 2:
                    if u % 2:
                        pe.wait_ge(y_ready_dve, u // 2)
                    else:
                        pe.wait_ge(y_ready_act, u // 2)
                for j in (0, 1):
                    for k in range(KD):
                        c = (2 * u + j) * P
                        ins = te.transpose(bank[6 + u % 2][:, (j * KD + k) * P:(j * KD + k + 1) * P],
                                           yT[:, k, c:c + P], ident[:])
                ins.then_inc(tY, 1)
    return nc


_INS = ["x", "ctx_1024", "mask_1xSxS2_ff0", "L0_xattn_kernel_q", "L0_xattn_bias_q", "L0_xattn_kernel_k",
        "L0_xattn_bias_k", "L0_xattn_kernel_v", "L0_xattn_bias_v", "L0_ffn_gate_w",
        "L0_ffn_shared_gate_w", "L0_ffn_shared_up_w", "L0_ffn_shared_down_w",
        "L0_ffn_routed_gate_w", "L0_ffn_routed_up_w", "L0_ffn_routed_down_w"]


def kernel(**inputs):
    import numpy as _np
    import concourse.bacc as _bacc
    from concourse import mybir as _mybir
    from concourse.bass_utils import run_bass_kernel_spmd as _run

    nc = _bacc.Bacc("TRN2", target_bir_lowering=False, num_devices=1)
    arrays, args = {}, []
    for name in _INS:
        a = _np.ascontiguousarray(inputs[name])
        arrays[f"in_{name}_dram"] = a
        args.append(nc.dram_tensor(f"in_{name}_dram", a.shape, _mybir.dt.from_np(a.dtype), kind="ExternalInput").ap())
    shape = inputs["x"].shape
    args.append(nc.dram_tensor("out_0_dram", shape, _mybir.dt.float32, kind="ExternalOutput").ap())
    build_cross_attention_moe(nc, *args)
    r = _run(nc, [arrays], core_ids=[0])
    return r.results[0]["out_0_dram"]
```

```python
from contextlib import ExitStack

import concourse.bass as bass
from concourse import mybir

ALU = mybir.AluOpType
ACT = mybir.ActivationFunctionType
AX = mybir.AxisListType
F32 = mybir.dt.float32
BF16 = mybir.dt.bfloat16
I32 = mybir.dt.int32
U32 = mybir.dt.uint32
P = 128


def build_cross_attention_moe(nc, x, ctx_in, mask, wq, bq, wk, bk, wv, bv, gate_w,
                              sh_gate_w, sh_up_w, sh_down_w, ex_gate_w, ex_up_w, ex_down_w, out):
    B, S, D = x.shape
    KV = ctx_in.shape[1]
    NE = gate_w.shape[1]
    FF = sh_gate_w.shape[1]
    T = B * S
    NT = T // P
    NTB = S // P
    NU = NT // 2
    KD = D // P
    KF = FF // P
    GT = 512
    NG = T // GT
    HALVES = 2
    LW = P // HALVES
    MAX_CHUNKS = NE + (T - NE) // LW
    MAX_PAIRS = (MAX_CHUNKS + 1) // 2
    FH, DH = FF // HALVES, D // HALVES
    RING = 8
    SORTED_RING = 4
    EPS = 1e-5
    SCALE = float(D) ** -0.5
    LOG_LW = LW.bit_length() - 1
    assert D == 256 and KD == 2 and GT == 4 * P and NE % RING == 0 and FF == 512
    assert 2 * MAX_PAIRS < P

    x_t = x.rearrange("b s d -> (b s) d").rearrange("(i p) d -> p i d", p=P)
    out_t = out.rearrange("b s d -> (b s) d").rearrange("(i p) d -> p i d", p=P)
    sorted_rows = nc.dram_tensor("sorted_rows", [T, D], F32, kind="Internal").ap()
    sorted_t = sorted_rows.rearrange("(i p) d -> p i d", p=P)
    slot_rows = nc.dram_tensor("slot_rows", [2 * MAX_PAIRS * LW, D], F32, kind="Internal").ap()
    slot_c = slot_rows.rearrange("(c t) (a d) -> c a t d", t=LW, a=HALVES)

    with ExitStack() as st:
        def sb(name, shape, dt=F32):
            return st.enter_context(nc.sbuf_tensor(name, shape, dt))

        def sem(name):
            return st.enter_context(nc.semaphore(name))

        bank = [st.enter_context(nc.psum_tensor(f"bank{i}", [P, 512], F32)) for i in range(8)]

        ident = sb("ident", [P, P])
        before = sb("before", [P, P], BF16)
        ones_bf = sb("ones_bf", [P, P], BF16)
        ones_row = sb("ones_row", [1, 2 * P])
        ones_scan = sb("ones_scan", [P, NE * NT])
        iota_row = sb("iota_row", [P, P])
        iota_p = sb("iota_p", [P, 1])
        power = sb("power", [P, NT])
        zeros = sb("zeros", [P, 1, D])
        h_place = sb("h_place", [P, 2 * KF * GT])
        taken = [0]

        def carve(parts, *shape):
            n = 1
            for s_ in shape:
                n *= s_
            a = taken[0]
            taken[0] += n
            assert taken[0] <= 2 * KF * GT
            view = h_place[0:parts, a:a + n]
            if len(shape) == 2:
                view = view.rearrange("p (a b) -> p a b", a=shape[0])
            return view

        h_s = h_place[:].rearrange("p (g m t) -> p g m t", g=2, m=KF)
        wq_sb = carve(P, KD, D)
        wk_sb = carve(P, KD, D)
        wv_sb = carve(P, KD, D)
        ctx_sb = carve(KV, B, D)
        ctxT = carve(P, KD, B * KV)
        wqT = carve(P, KD, D)
        kT = carve(P, KD, B * KV)
        bq_wide = carve(P, KD, P)
        mask_sb = carve(P, NTB, KV)
        bq_row = sb("bq_row", [1, D])
        bk_row = sb("bk_row", [1, D])
        bv_row = sb("bv_row", [1, D])
        v_sb = sb("v_sb", [KV, B, D])
        qk = sb("qk", [P, KD, B * KV])
        bias_k = sb("bias_k", [P, B * KV])
        mask_b = sb("mask_b", [P, B, NTB, KV])
        x1 = sb("x1", [P, NT, D])
        xs_flat = sb("xs_flat", [P, KD * (T + LW)])
        xn = xs_flat[:, 0:NT * D].rearrange("p (i d) -> p i d", i=NT)
        xsT = xs_flat[:].rearrange("p (k t) -> p k t", k=KD)
        pairT = sb("pairT", [P, 2, 2, KD, P])
        tot_first = pairT[:].rearrange("p a b c d -> p (a b c d)").rearrange("p (w e i) -> p w e i", w=2, e=NE)
        tot, first = tot_first[:, 0], tot_first[:, 1]
        probs = sb("probs", [P, 6, KV])
        pT = sb("pT", [KV, 2, 2, P])
        stats1 = sb("stats1", [P, NT, 6])
        stats2 = sb("stats2", [P, NT, 6])
        mv1 = sb("mv1", [P, NT, 2])
        mv2 = sb("mv2", [P, NT, 2])
        var1 = sb("var1", [P, NT])
        var2 = sb("var2", [P, NT])
        rstd1 = sb("rstd1", [P, NT])
        shift1 = sb("shift1", [P, NT])
        rstd2 = sb("rstd2", [P, NT])
        nmax = sb("nmax", [P, NT])
        psum_p = sb("psum_p", [P, NT])
        rsum = sb("rsum", [P, NT])
        xnT = sb("xnT", [P, KD, T])
        gate_sb = sb("gate_sb", [P, KD, NE])
        top8 = sb("top8", [P, NT, 8])
        idx8 = sb("idx8", [P, NT, 8], U32)
        half_tanh = sb("half_tanh", [P, NT])
        score = sb("score", [P, NT])
        expert_f = sb("expert_f", [P, NT])
        onehot = sb("onehot", [P, NT, NE], BF16)
        place = mask_b[:].rearrange("p b i k -> p (b i k)")[:, 0:NT * NE].rearrange("p (i e) -> p i e", i=NT)
        pos_f = sb("pos_f", [P, NT])
        pos = sb("pos", [P, NT], I32)
        count_f = sb("count_f", [P, NE])
        chunk_i = sb("chunk_i", [P, NE], I32)
        chunk_f = sb("chunk_f", [P, NE])
        chunk_cum = sb("chunk_cum", [P, NE])
        adjust = sb("adjust", [P, NE])
        padding = sb("padding", [P, NE])
        slot_f = sb("slot_f", [P, NT])
        slot_i = sb("slot_i", [P, NT], I32)
        done_before = sb("done_before", [P, NE])
        begin_f = sb("begin_f", [P, 1])
        begin = sb("begin", [1, P], I32)
        chunk_n = sb("chunk_n", [1, NE], I32)
        chunk_first = sb("chunk_first", [1, NE], I32)
        pair_f = sb("pair_f", [1, 2])
        pair_n = sb("pair_n", [1, 2], I32)
        chunk_end = sb("chunk_end", [1, NE], I32)
        shg = sb("shg", [P, KD, FF])
        shu = sb("shu", [P, KD, FF])
        shd = sb("shd", [P, KF, D])
        ring_gu = sb("ring_gu", [P, RING, 2, KD, FF])
        ring_d = sb("ring_d", [P, RING, KF, D])
        taken[0] = 0
        x_c = carve(P, KD, LW)
        h_r = carve(P, FH)
        hT = carve(P, KF // HALVES, P)
        y_c = carve(P, 2, DH)
        y_t = xnT[:].rearrange("p k t -> p (k t)").rearrange("p (i d) -> p i d", i=NT)
        sorted_own = sb("sorted_own", [P, 4, D])
        sorted_pair = [sorted_own[:, 0:2], sorted_own[:, 2:4]] + [
            pairT[:, b].rearrange("p j k c -> p (j k c)").rearrange("p (t d) -> p t d", t=2) for b in (0, 1)]

        x_in = [sem(f"x_in{g}") for g in range(4)]
        ctx_w_in = sem("ctx_w_in")
        mask_in = sem("mask_in")
        gate_in = sem("gate_in")
        shared_in = sem("shared_in")
        gu_in = [sem(f"gu_in{s}") for s in range(RING)]
        d_in = [sem(f"d_in{s}") for s in range(RING)]
        zeros_out = sem("zeros_out")
        scattered = sem("scattered")
        sorted_in = [sem(f"sorted_in{g}") for g in range(SORTED_RING)]
        y_stored = [sem(f"y_stored{q}") for q in (0, 1)]
        y_in = [sem(f"y_in{u}") for u in range(NU)]
        out_done = sem("out_done")
        pool_step = sem("pool_step")
        dve_step = sem("dve_step")
        consts = sem("consts")
        prep_pe = sem("prep_pe")
        prep_act = sem("prep_act")
        prep_dve = sem("prep_dve")
        ln1_stats = sem("ln1_stats")
        rstd1_ready = sem("rstd1_ready")
        xn_ready = sem("xn_ready")
        tA = sem("tA")
        pairT_ready = sem("pairT_ready")
        logits_ready = sem("logits_ready")
        s_ready = sem("s_ready")
        p_ready = sem("p_ready")
        tP = sem("tP")
        pT_ready = sem("pT_ready")
        av_ready = sem("av_ready")
        x1_ready = sem("x1_ready")
        ln2_stats = sem("ln2_stats")
        rstd2_ready = sem("rstd2_ready")
        xn2_ready = sem("xn2_ready")
        tE = sem("tE")
        xnT_ready = sem("xnT_ready")
        gate_ready = sem("gate_ready")
        top_ready = sem("top_ready")
        tanh_ready = sem("tanh_ready")
        xs_ready = sem("xs_ready")
        onehot_ready = sem("onehot_ready")
        ranks_ready = sem("ranks_ready")
        pos_ready = sem("pos_ready")
        slot_ready = sem("slot_ready")
        begin_done = sem("begin_done")
        tX = sem("tX")
        xsT_ready = sem("xsT_ready")
        table_ready = sem("table_ready")
        sh_gu = sem("sh_gu")
        sh_silu = sem("sh_silu")
        sh_h = sem("sh_h")
        sh_down = sem("sh_down")
        residual_ready = sem("residual_ready")
        x_ready = sem("x_ready")
        g_done = sem("g_done")
        u_done = sem("u_done")
        silu_done = sem("silu_done")
        h_ready = sem("h_ready")
        hT_done = sem("hT_done")
        hT_ready = sem("hT_ready")
        down_done = sem("down_done")
        y_ready = sem("y_ready")
        sum_ready = sem("sum_ready")
        pool_waited = sem("pool_waited")

        PARTS = "p (t n) -> p t n"
        FLAT = "p a b -> p (a b)"
        FREE1, FREE2, FREE_H = 1, 2, 4

        def pair_count(eng):
            return eng.value_load(pair_n[0:1, 0:1], min_val=NE // 2, max_val=MAX_PAIRS)

        block = st.enter_context(nc.Block())

        @block.sync
        def _(sp):
            def load_expert(e, s):
                sp.dma_start(ring_gu[:, s, 0], ex_gate_w[bass.ds(e, 1)].rearrange("a (k p) f -> p (a k) f", p=P)).then_inc(gu_in[s], 16)
                sp.dma_start(ring_gu[:, s, 1], ex_up_w[bass.ds(e, 1)].rearrange("a (k p) f -> p (a k) f", p=P)).then_inc(gu_in[s], 16)
                sp.dma_start(ring_d[:, s], ex_down_w[bass.ds(e, 1)].rearrange("a (m p) d -> p (a m) d", p=P)).then_inc(d_in[s], 16)

            sp.dma_start(x1[:, 0:4], x_t[:, 0:4]).then_inc(x_in[0], 16)
            sp.dma_start(ctx_sb, ctx_in.rearrange("b k d -> k b d")).then_inc(ctx_w_in, 16)
            for dst, src in ((wk_sb, wk), (wq_sb, wq), (wv_sb, wv)):
                sp.dma_start(dst, src.rearrange("(k p) d -> p k d", p=P)).then_inc(ctx_w_in, 16)
            for dst, src in ((bq_row, bq), (bk_row, bk), (bv_row, bv)):
                sp.dma_start(dst[:], src.rearrange("(a d) -> a d", a=1)).then_inc(ctx_w_in, 16)
            sp.dma_start(mask_sb, mask[0].rearrange("(i p) k -> p i k", p=P)).then_inc(mask_in, 16)
            for g in range(1, 4):
                sp.dma_start(x1[:, 4 * g:4 * g + 4], x_t[:, 4 * g:4 * g + 4]).then_inc(x_in[g], 16)
            sp.dma_start(gate_sb[:], gate_w.rearrange("(k p) e -> p k e", p=P)).then_inc(gate_in, 16)
            sp.dma_start(shg[:], sh_gate_w.rearrange("(k p) f -> p k f", p=P)).then_inc(shared_in, 16)
            sp.dma_start(shu[:], sh_up_w.rearrange("(k p) f -> p k f", p=P)).then_inc(shared_in, 16)
            sp.dma_start(shd[:], sh_down_w.rearrange("(m p) d -> p m d", p=P)).then_inc(shared_in, 16)
            for s in range(RING):
                load_expert(s, s)
            sp.wait_ge(scattered, 16 * NT)
            sp.wait_ge(slot_ready, 2)
            for u in range(NU):
                b = u % SORTED_RING
                if u >= SORTED_RING:
                    sp.wait_ge(tX, u - SORTED_RING + 1)
                sp.dma_start(sorted_pair[b], sorted_t[:, 2 * u:2 * u + 2]).then_inc(sorted_in[b], 16)
            sp.wait_ge(table_ready, 3)
            with sp.Fori(0, NE // RING - 1) as it:
                for s in range(RING):
                    e = RING * it + s
                    end = sp.value_load(chunk_end[0:1, bass.ds(e, 1)], min_val=1, max_val=MAX_CHUNKS)
                    sp.wait_ge(down_done, HALVES * end)
                    load_expert(e + RING, s)
            for u in range(NU):
                sp.wait_ge(sum_ready, u + 1)
                sp.dma_start(out_t[:, 2 * u:2 * u + 2], x1[:, 2 * u:2 * u + 2]).then_inc(out_done, 16)
            sp.wait_ge(out_done, 16 * NU)

        @block.gpsimd
        def _(pool):
            steps = [0]

            def step(ins):
                steps[0] += 1
                ins.then_inc(pool_step, 1)
                pool.wait_ge(pool_step, steps[0])

            g_ = nc.gpsimd
            step(g_.memset(ident[:], 0.0))
            g_.affine_select(out=ident[:], in_=ident[:], compare_op=ALU.not_equal, fill=1.0, base=0,
                             pattern=[[-1, P]], channel_multiplier=1).then_inc(consts, 1)
            g_.memset(ones_row[:], 1.0).then_inc(consts, 1)
            g_.memset(power[:], -0.5).then_inc(consts, 1)
            step(g_.memset(zeros[:], 0.0))
            g_.dma_start(slot_rows[NE * LW:].rearrange("(p r) d -> p r d", p=P),
                         zeros[:].to_broadcast([P, (2 * MAX_PAIRS - NE) * LW // P, D])).then_inc(zeros_out, 16)
            pool.wait_ge(consts, 3)

            for g in range(4):
                a = 4 * g
                pool.wait_ge(ln1_stats, 4 * g + 4)
                step(g_.tensor_scalar(var1[:, a:a + 4], mv1[:, a:a + 4, 1], EPS, None, ALU.add))
                step(g_.tensor_tensor(rstd1[:, a:a + 4], var1[:, a:a + 4], power[:, 0:4], ALU.pow))
                step(g_.tensor_tensor(shift1[:, a:a + 4], mv1[:, a:a + 4, 0], rstd1[:, a:a + 4], ALU.mult))
                g_.tensor_scalar(shift1[:, a:a + 4], shift1[:, a:a + 4], -1.0, None, ALU.mult).then_inc(rstd1_ready, 1)

            g_.memset(ones_bf[:], 1.0).then_inc(consts, 1)
            step(g_.memset(before[:], 0.0))
            g_.affine_select(out=before[:], in_=before[:], compare_op=ALU.is_ge, fill=1.0, base=0,
                             pattern=[[-1, P]], channel_multiplier=1).then_inc(consts, 1)
            g_.iota(iota_row[:], pattern=[[1, P]], base=0, channel_multiplier=0,
                    allow_small_or_imprecise_dtypes=True).then_inc(consts, 1)
            g_.iota(iota_p[:], pattern=[[0, 1]], base=0, channel_multiplier=1,
                    allow_small_or_imprecise_dtypes=True).then_inc(consts, 1)
            g_.memset(ones_scan[:], 1.0).then_inc(consts, 1)

            def rstd_2(u):
                a = 2 * u
                pool.wait_ge(ln2_stats, 2 * u + 2)
                step(g_.tensor_scalar(var2[:, a:a + 2], mv2[:, a:a + 2, 1], EPS, None, ALU.add))
                g_.tensor_tensor(rstd2[:, a:a + 2], var2[:, a:a + 2], power[:, 0:2], ALU.pow).then_inc(rstd2_ready, 1)

            def scaled(u):
                a = 2 * u
                pool.wait_ge(tanh_ready, u + 1)
                step(g_.tensor_scalar(score[:, a:a + 2], half_tanh[:, a:a + 2], 0.5, 0.5, ALU.mult, ALU.add))
                pool.wait_ge(tE, u + 1)
                for i in (a, a + 1):
                    g_.tensor_scalar(xn[:, i], xn[:, i], score[:, i:i + 1], None, ALU.mult).then_inc(xs_ready, 1)

            for t in range(4, NU + 7):
                if 0 <= t - 7 < NU:
                    scaled(t - 7)
                if 0 <= t - 4 < NU:
                    rstd_2(t - 4)

            pool.wait_ge(xs_ready, NT)
            pool.wait_ge(pos_ready, 1)
            for i in range(NT):
                g_.indirect_dma_start(
                    out=sorted_rows, out_offset=bass.IndirectOffsetOnAxis(ap=pos[:, i:i + 1], axis=0),
                    in_=xn[:, i, :], in_offset=None).then_inc(scattered, 16)
            pool.wait_ge(scattered, 16 * NT)
            g_.memset(xsT[:, :, T:T + LW], 0.0).then_inc(xsT_ready, 1)

            pool.wait_ge(table_ready, 3)
            pairs = pair_count(pool)
            for q in (0, 1):
                pool.wait_ge(y_stored[q], 16 * pairs)
            pool.sem_inc(pool_waited, 1)
            for i in range(NT):
                g_.indirect_dma_start(
                    out=y_t[:, i, :], out_offset=None, in_=slot_rows,
                    in_offset=bass.IndirectOffsetOnAxis(ap=slot_i[:, i:i + 1], axis=0)).then_inc(y_in[i // 2], 16)

        @block.vector
        def _(dve):
            v = nc.vector
            steps = [0]

            def step(ins):
                steps[0] += 1
                ins.then_inc(dve_step, 1)
                dve.wait_ge(dve_step, steps[0])

            def layer_stats(u, stats, mv, done):
                a = 2 * u
                steps[0] += 1
                v.bn_stats(stats[:, a], x1[:, a]).then_inc(dve_step, 1)
                step(v.bn_stats(stats[:, a + 1], x1[:, a + 1]))
                for i in (a, a + 1):
                    v.bn_aggr(mv[:, i], stats[:, i]).then_inc(done, 1)

            def stage_mask(u):
                a = 2 * u
                dve.wait_ge(logits_ready, u + 1)
                c = 2 * (u % 3)
                if u >= 3:
                    dve.wait_ge(tP, u - 2)
                step(v.tensor_tensor(probs[:, c:c + 2], bank[1][:, 0:2 * KV].rearrange(PARTS, t=2),
                                     mask_b[:, a // NTB, a % NTB:a % NTB + 2], ALU.add))
                v.tensor_reduce(nmax[:, a:a + 2], probs[:, c:c + 2], AX.X, ALU.max, negate=True).then_inc(s_ready, 1)

            def stage_x1(u):
                a = 2 * u
                dve.wait_ge(p_ready, 2 * u + 2)
                step(v.reciprocal(rsum[:, a:a + 2], psum_p[:, a:a + 2]))
                dve.wait_ge(av_ready, u + 1)
                dve.wait_ge(xn_ready, 2 * u + 2)
                for j in (0, 1):
                    v.scalar_tensor_tensor(out=x1[:, a + j], in0=bank[3][:, j * D:(j + 1) * D],
                                           scalar=rsum[:, a + j:a + j + 1], in1=x1[:, a + j],
                                           op0=ALU.mult, op1=ALU.add).then_inc(x1_ready, 1)
                dve.wait_ge(x1_ready, 2 * u + 2)
                layer_stats(u, stats2, mv2, ln2_stats)

            def stage_xn2(u):
                a = 2 * u
                dve.wait_ge(rstd2_ready, u + 1)
                dve.wait_ge(tA, u + 1)
                for i in (a, a + 1):
                    v.tensor_scalar(xn[:, i], x1[:, i], mv2[:, i, 0:1], rstd2[:, i:i + 1],
                                    ALU.subtract, ALU.mult).then_inc(xn2_ready, 1)

            def stage_top(u):
                a = 2 * u
                dve.wait_ge(gate_ready, u + 1)
                for j in (0, 1):
                    g = bank[5][:, j * NE:(j + 1) * NE]
                    step(v.max(top8[:, a + j], g))
                    v.max_index(idx8[:, a + j], top8[:, a + j], g).then_inc(top_ready, 1)

            for u in (0, 1):
                dve.wait_ge(x_in[0], 16)
                layer_stats(u, stats1, mv1, ln1_stats)
            dve.wait_ge(prep_pe, 1)
            v.tensor_copy(ctxT.rearrange("p k n -> p (k n)"), bank[6][:, 0:KD * B * KV]).then_inc(prep_dve, 1)
            dve.wait_ge(prep_pe, 4)
            v.tensor_copy(kT.rearrange("p k n -> p (k n)"), bank[5][:, 0:KD * B * KV]).then_inc(prep_dve, 1)
            for u in range(2, 4):
                dve.wait_ge(x_in[u // 2], 16)
                layer_stats(u, stats1, mv1, ln1_stats)
            dve.wait_ge(prep_pe, 6)
            step(v.tensor_scalar(bias_k[:], bank[1][:, 0:B * KV], SCALE, None, ALU.mult))
            dve.wait_ge(mask_in, 16)
            for b in range(B):
                v.tensor_tensor(mask_b[:, b], mask_sb,
                                bias_k[:, b * KV:(b + 1) * KV].rearrange("p (a k) -> p a k", a=1).to_broadcast([P, NTB, KV]),
                                ALU.add).then_inc(prep_dve, 1)
            for u in range(4, NU):
                dve.wait_ge(x_in[u // 2], 16)
                layer_stats(u, stats1, mv1, ln1_stats)
            dve.wait_ge(prep_dve, 4)
            for t in range(2, NU + 6):
                if 0 <= t - 5 < NU:
                    stage_xn2(t - 5)
                if 0 <= t - 4 < NU:
                    stage_x1(t - 4)
                if 0 <= t - 6 < NU:
                    stage_top(t - 6)
                if 0 <= t - 2 < NU:
                    stage_mask(t - 2)

            dve.wait_ge(top_ready, NT)
            dve.wait_ge(consts, 8)
            step(v.tensor_copy(expert_f[:], idx8[:, :, 0]))
            v.tensor_tensor(onehot[:], iota_row[:, 0:NE].rearrange("p (a e) -> p a e", a=1).to_broadcast([P, NT, NE]),
                            expert_f[:].rearrange("p (i a) -> p i a", a=1).to_broadcast([P, NT, NE]),
                            ALU.is_equal).then_inc(onehot_ready, 1)
            dve.wait_ge(onehot_ready, 1)
            dve.wait_ge(ranks_ready, 1)
            step(v.tensor_copy(tot, bank[7][:].rearrange("p (i e) -> p e i", e=NE)))
            step(v.tensor_tensor_scan(first.rearrange(FLAT), ones_scan[:], tot.rearrange(FLAT), 0.0,
                                      ALU.mult, ALU.add))
            step(v.tensor_tensor(first, first, tot, ALU.subtract))
            step(v.tensor_tensor(place, bank[6][:].rearrange("p (i e) -> p i e", e=NE),
                                 first.rearrange("p e i -> p i e"), ALU.add))
            step(v.tensor_tensor(place, place, onehot[:], ALU.mult))
            step(v.tensor_reduce(pos_f[:], place, AX.X, ALU.add))
            v.tensor_copy(pos[:], pos_f[:]).then_inc(pos_ready, 1)
            step(v.tensor_reduce(count_f[:], tot, AX.X, ALU.add))
            step(v.tensor_scalar(chunk_f[:], count_f[:], 1.0, LW - 1.0, ALU.max, ALU.add))
            step(v.tensor_copy(chunk_i[:], chunk_f[:]))
            step(v.tensor_scalar(chunk_i[:], chunk_i[:], LOG_LW, None, ALU.arith_shift_right))
            step(v.tensor_copy(chunk_f[:], chunk_i[:]))
            steps[0] += 1
            v.tensor_tensor_scan(chunk_cum[:], ones_scan[:, 0:NE], chunk_f[:], 0.0, ALU.mult, ALU.add).then_inc(dve_step, 1)
            step(v.scalar_tensor_tensor(out=padding[:], in0=chunk_f[:], scalar=float(LW), in1=count_f[:],
                                        op0=ALU.mult, op1=ALU.subtract))
            step(v.tensor_tensor_scan(adjust[:], ones_scan[:, 0:NE], padding[:], 0.0, ALU.mult, ALU.add))
            step(v.tensor_tensor(adjust[:], adjust[:], padding[:], ALU.subtract))
            step(v.tensor_tensor(place, onehot[:],
                                 adjust[:].rearrange("p (a e) -> p a e", a=1).to_broadcast([P, NT, NE]), ALU.mult))
            step(v.tensor_reduce(slot_f[:], place, AX.X, ALU.add))
            step(v.tensor_tensor(slot_f[:], slot_f[:], pos_f[:], ALU.add))
            v.tensor_copy(slot_i[:], slot_f[:]).then_inc(slot_ready, 1)
            step(v.tensor_scalar(done_before[:], chunk_cum[:], iota_p[:], None, ALU.is_le))
            step(v.tensor_tensor(done_before[:], done_before[:], padding[:], ALU.mult))
            step(v.tensor_reduce(begin_f[:], done_before[:], AX.X, ALU.add))
            v.scalar_tensor_tensor(out=begin_f[:], in0=iota_p[:], scalar=float(LW), in1=begin_f[:],
                                   op0=ALU.mult, op1=ALU.subtract).then_inc(slot_ready, 1)
            step(v.tensor_scalar(pair_f[:, 0:1], chunk_cum[0:1, NE - 1:NE], 1.0, None, ALU.add))
            step(v.tensor_copy(pair_n[:, 0:1], pair_f[:, 0:1]))
            step(v.tensor_scalar(pair_n[:, 0:1], pair_n[:, 0:1], 1, None, ALU.arith_shift_right))
            step(v.tensor_copy(pair_f[:, 0:1], pair_n[:, 0:1]))
            step(v.scalar_tensor_tensor(out=pair_f[:, 1:2], in0=pair_f[:, 0:1], scalar=2.0, in1=chunk_cum[0:1, NE - 1:NE],
                                        op0=ALU.mult, op1=ALU.subtract))
            step(v.tensor_copy(pair_n[:, 1:2], pair_f[:, 1:2]))
            v.tensor_copy(chunk_n[:], chunk_f[0:1]).then_inc(table_ready, 1)
            v.tensor_copy(chunk_end[:], chunk_cum[0:1]).then_inc(table_ready, 1)
            v.tensor_tensor(chunk_first[:], chunk_cum[0:1], chunk_f[0:1], ALU.subtract).then_inc(table_ready, 1)

            with dve.Fori(0, NG // 2) as it:
                def shared_h(g2, m):
                    n = KF * g2 + m
                    dve.wait_ge(sh_silu, 2 * KF * it + n + 1)
                    v.tensor_tensor(h_s[:, g2, m], h_s[:, g2, m], bank[2 + n % 2][:], ALU.mult).then_inc(sh_h, 1)

                def shared_residual(w):
                    dve.wait_ge(sh_down, 4 * it + w + 1 + FREE_H)
                    rows = x1[:, bass.ds(2 * (4 * it + w), 2)]
                    v.tensor_tensor(rows, bank[4 + w % 2][:].rearrange(PARTS, t=2), rows, ALU.add).then_inc(residual_ready, 1)

                for m in range(KF):
                    shared_h(0, m)
                shared_h(1, 0)
                shared_h(1, 1)
                shared_residual(0)
                shared_residual(1)
                shared_h(1, 2)
                shared_h(1, 3)
                shared_residual(2)
                shared_residual(3)

            dve.wait_ge(begin_done, 1)
            step(v.tensor_scalar(begin[:], bank[0][0:1, 0:P], float(T), None, ALU.min))

            def take_x(c):
                col = dve.value_load(begin[0:1, bass.ds(c, 1)], min_val=0, max_val=T)
                dve.wait_ge(u_done, HALVES * c)
                v.tensor_copy(x_c, xsT[:, :, bass.ds(col, LW)]).then_inc(x_ready, 1)

            def gated(c):
                dve.wait_ge(silu_done, c + 1)
                dve.wait_ge(u_done, HALVES * (c + 1))
                v.tensor_tensor(h_r, h_r, bank[1][:, 0:FH], ALU.mult).then_inc(h_ready, 1)

            def take_y(c, q, n_stored):
                dve.wait_ge(down_done, HALVES * (c + 1))
                if n_stored is not None:
                    dve.wait_ge(y_stored[q], 16 * n_stored)
                v.tensor_copy(y_c[:, q], bank[4][:, 0:DH]).then_inc(y_ready, 1)

            dve.wait_ge(xsT_ready, NU + 1)
            pairs = pair_count(dve)
            take_x(0)
            gated(0)
            take_x(1)
            gated(1)
            take_x(2)
            take_y(0, 0, None)
            with dve.Fori(1, pairs) as p:
                gated(2 * p)
                take_x(2 * p + 1)
                take_y(2 * p - 1, 1, p - 1)
                gated(2 * p + 1)
                take_x(2 * p + 2)
                take_y(2 * p, 0, p)
            dve.wait_ge(down_done, HALVES * 2 * pairs)
            dve.wait_ge(y_stored[0], 16 * pairs)
            v.tensor_copy(y_c[:, 1], bank[4][:, 0:DH]).then_inc(y_ready, 1)
            for u in range(NU):
                dve.wait_ge(y_in[u], 32)
                v.tensor_tensor(x1[:, 2 * u:2 * u + 2], x1[:, 2 * u:2 * u + 2], y_t[:, 2 * u:2 * u + 2], ALU.add).then_inc(sum_ready, 1)

        @block.scalar
        def _(act):
            a_ = nc.scalar

            act.wait_ge(prep_pe, 2)
            a_.copy(wqT.rearrange("p k n -> p (k n)"), bank[7][:]).then_inc(prep_act, 1)
            act.wait_ge(prep_pe, 3)
            a_.copy(bq_wide.rearrange("p k n -> p (k n)"), bank[4][:, 0:KD * P]).then_inc(prep_act, 1)

            def normalise(u):
                act.wait_ge(rstd1_ready, u // 2 + 1)
                for i in (0, 1):
                    n = 2 * u + i
                    a_.activation(xn[:, n], x1[:, n], ACT.Identity, bias=shift1[:, n:n + 1],
                                  scale=rstd1[:, n:n + 1]).then_inc(xn_ready, 1)

            def keep_normT(u):
                act.wait_ge(tA, u + 1)
                if u >= 2:
                    act.wait_ge(logits_ready, u - 1)
                a_.copy(pairT[:, u % 2].rearrange("p j k c -> p (j k c)"), bank[0][:]).then_inc(pairT_ready, 1)

            def exponentials(u):
                act.wait_ge(s_ready, u + 1)
                for i in (2 * u, 2 * u + 1):
                    p_i = probs[:, 2 * (u % 3) + i % 2]
                    a_.activation(p_i, p_i, ACT.Exp, bias=nmax[:, i:i + 1],
                                  accum_out=psum_p[:, i:i + 1]).then_inc(p_ready, 1)

            def keep_probsT(u):
                act.wait_ge(tP, u + 1)
                if u >= 2:
                    act.wait_ge(av_ready, u - 1)
                a_.copy(pT[:, u % 2].rearrange("p j c -> p (j c)"), bank[2][0:KV, 0:2 * P]).then_inc(pT_ready, 1)

            def keep_norm2T(u):
                act.wait_ge(tE, u + 1)
                a_.copy(xnT[:, :, 2 * P * u:2 * P * (u + 1)].rearrange("p k (j c) -> p j k c", j=2),
                        bank[4][:].rearrange("p (j k c) -> p j k c", j=2, k=KD)).then_inc(xnT_ready, 1)

            def top_tanh(u):
                act.wait_ge(top_ready, 2 * u + 2)
                a_.activation(half_tanh[:, 2 * u:2 * u + 2], top8[:, 2 * u:2 * u + 2, 0], ACT.Tanh,
                              scale=0.5).then_inc(tanh_ready, 1)

            normalise(0)
            act.wait_ge(prep_pe, 5)
            a_.copy(v_sb[:].rearrange("p k n -> p (k n)"), bank[3][0:KV, 0:B * D]).then_inc(prep_act, 1)
            act.wait_ge(prep_pe, 7)
            a_.mul(qk[:].rearrange("p k n -> p (k n)"), bank[2][:, 0:KD * B * KV], SCALE).then_inc(prep_act, 1)

            for t in range(1, NU + 8):
                if 0 <= t - 3 < NU:
                    exponentials(t - 3)
                if t < NU:
                    normalise(t)
                if 0 <= t - 1 < NU:
                    keep_normT(t - 1)
                if 0 <= t - 5 < NU:
                    keep_norm2T(t - 5)
                if 0 <= t - 3 < NU:
                    keep_probsT(t - 3)
                if 0 <= t - 7 < NU:
                    top_tanh(t - 7)

            with act.Fori(0, NG // 2) as it:
                for n in range(2 * KF):
                    act.wait_ge(sh_gu, 2 * KF * it + n + 1)
                    if n % KF == 0:
                        act.wait_ge(sh_down, 4 * it + 2 * (n // KF) - 4 + 2 + FREE_H)
                    a_.activation(h_s[:, n // KF, n % KF], bank[n % 2][:], ACT.Silu).then_inc(sh_silu, 1)

            act.wait_ge(xsT_ready, 1)
            for u in range(NU):
                act.wait_ge(tX, u + 1)
                a_.copy(xsT[:, :, 2 * P * u:2 * P * (u + 1)].rearrange("p k (j c) -> p j k c", j=2),
                        bank[6 + u % 2][:].rearrange("p (j k c) -> p j k c", j=2, k=KD)).then_inc(xsT_ready, 1)

            def silu(c):
                act.wait_ge(g_done, HALVES * (c + 1))
                act.wait_ge(hT_done, c)
                a_.activation(h_r, bank[0][:, 0:FH], ACT.Silu).then_inc(silu_done, 1)

            def keep_hT(c):
                act.wait_ge(hT_done, c + 1)
                act.wait_ge(down_done, HALVES * c)
                a_.copy(hT.rearrange(FLAT), bank[3][:, 0:FH]).then_inc(hT_ready, 1)

            def store_y(c, q):
                act.wait_ge(y_ready, c + 1 + FREE1)
                act.dma_start(slot_c[bass.ds(c, 1)].rearrange("c a t d -> (c a) t d"), y_c[:, q]).then_inc(y_stored[q], 16)

            act.wait_ge(table_ready, 3)
            pairs = pair_count(act)
            silu(0)
            keep_hT(0)
            silu(1)
            keep_hT(1)
            act.wait_ge(zeros_out, 16)
            store_y(0, 0)
            with act.Fori(1, pairs) as p:
                silu(2 * p)
                keep_hT(2 * p)
                store_y(2 * p - 1, 1)
                silu(2 * p + 1)
                keep_hT(2 * p + 1)
                store_y(2 * p, 0)
            last = pairs * 2 - 1
            act.wait_ge(y_ready, 2 * pairs + FREE1)
            act.dma_start(slot_c[bass.ds(last, 1)].rearrange("c a t d -> (c a) t d"), y_c[:, 1]).then_inc(y_stored[1], 16)

        @block.tensor
        def _(pe):
            te = nc.tensor
            for s_, n in ((sh_h, FREE2), (sh_down, FREE_H), (y_ready, FREE1)):
                pe.sem_inc(s_, n)

            pe.wait_ge(consts, 3)
            pe.wait_ge(ctx_w_in, 16 * 7)
            for k in range(KD):
                for b in range(B):
                    c = (k * B + b) * KV
                    ins = te.transpose(bank[6][:, c:c + KV], ctx_sb[:, b, k * P:(k + 1) * P], ident[0:KV, 0:KV])
            ins.then_inc(prep_pe, 1)
            for dk in range(KD):
                for ik in range(KD):
                    ins = te.transpose(bank[7][:, dk * D + ik * P:dk * D + (ik + 1) * P],
                                       wq_sb[:, ik, dk * P:(dk + 1) * P], ident[:])
            ins.then_inc(prep_pe, 1)
            for dk in range(KD):
                ins = te.matmul(bank[4][:, dk * P:(dk + 1) * P], bq_row[:, dk * P:(dk + 1) * P],
                                ones_row[:, 0:P], start=True, stop=True)
            ins.then_inc(prep_pe, 1)
            pe.wait_ge(prep_dve, 1)
            for dk in range(KD):
                o = bank[5][:, dk * B * KV:(dk + 1) * B * KV]
                for ik in range(KD):
                    te.matmul(o, wk_sb[:, ik, dk * P:(dk + 1) * P], ctxT[:, ik], start=(ik == 0), stop=False)
                ins = te.matmul(o, bk_row[:, dk * P:(dk + 1) * P], ones_row[:, 0:B * KV], start=False, stop=True)
            ins.then_inc(prep_pe, 1)
            for b in range(B):
                o = bank[3][0:KV, b * D:(b + 1) * D]
                for ik in range(KD):
                    te.matmul(o, ctxT[:, ik, b * KV:(b + 1) * KV], wv_sb[:, ik], start=(ik == 0), stop=False)
                ins = te.matmul(o, ones_row[:, 0:KV], bv_row[:], start=False, stop=True)
            ins.then_inc(prep_pe, 1)
            pe.wait_ge(prep_dve, 2)
            pe.wait_ge(prep_act, 2)
            for dk in range(KD):
                ins = te.matmul(bank[1][:, 0:B * KV], bq_wide[:, dk], kT[:, dk], start=(dk == 0), stop=(dk == KD - 1))
            ins.then_inc(prep_pe, 1)
            for ik in range(KD):
                for dk in range(KD):
                    ins = te.matmul(bank[2][:, ik * B * KV:(ik + 1) * B * KV], wqT[:, dk, ik * P:(ik + 1) * P],
                                    kT[:, dk], start=(dk == 0), stop=(dk == KD - 1))
            ins.then_inc(prep_pe, 1)

            def transpose_pair(dst, src, a, done):
                for j in (0, 1):
                    for k in range(KD):
                        c = (j * KD + k) * P
                        ins = te.transpose(dst[:, c:c + P], src[:, a + j, k * P:(k + 1) * P], ident[:])
                ins.then_inc(done, 1)

            def norm_transposes(u):
                pe.wait_ge(xn_ready, 2 * u + 2)
                if u:
                    pe.wait_ge(pairT_ready, u)
                transpose_pair(bank[0], xn, 2 * u, tA)

            def logits(u):
                pe.wait_ge(pairT_ready, u + 1)
                if u:
                    pe.wait_ge(s_ready, u)
                b = 2 * u // NTB
                for j in (0, 1):
                    for k in range(KD):
                        ins = te.matmul(bank[1][:, j * KV:(j + 1) * KV], pairT[:, u % 2, j, k],
                                        qk[:, k, b * KV:(b + 1) * KV], start=(k == 0), stop=(k == KD - 1))
                ins.then_inc(logits_ready, 1)

            def probs_transposes(u):
                pe.wait_ge(p_ready, 2 * u + 2)
                if u:
                    pe.wait_ge(pT_ready, u)
                for j in (0, 1):
                    ins = te.transpose(bank[2][0:KV, j * P:(j + 1) * P], probs[:, 2 * (u % 3) + j], ident[:])
                ins.then_inc(tP, 1)

            def attend(u):
                pe.wait_ge(pT_ready, u + 1)
                if u:
                    pe.wait_ge(x1_ready, 2 * u)
                for j in (0, 1):
                    ins = te.matmul(bank[3][:, j * D:(j + 1) * D], pT[:, u % 2, j], v_sb[:, 2 * u // NTB],
                                    start=True, stop=True)
                ins.then_inc(av_ready, 1)

            def norm2_transposes(u):
                pe.wait_ge(xn2_ready, 2 * u + 2)
                if u:
                    pe.wait_ge(xnT_ready, u)
                transpose_pair(bank[4], xn, 2 * u, tE)

            def gates(u):
                pe.wait_ge(xnT_ready, u + 1)
                if u:
                    pe.wait_ge(top_ready, 2 * u)
                for j in (0, 1):
                    for k in range(KD):
                        ins = te.matmul(bank[5][:, j * NE:(j + 1) * NE], xnT[:, k, (2 * u + j) * P:(2 * u + j + 1) * P],
                                        gate_sb[:, k], start=(k == 0), stop=(k == KD - 1))
                ins.then_inc(gate_ready, 1)

            pe.wait_ge(prep_act, 4)
            pe.wait_ge(prep_dve, 4)
            pe.wait_ge(gate_in, 16)
            for t in range(1, NU + 6):
                if 0 <= t - 4 < NU:
                    attend(t - 4)
                if 0 <= t - 6 < NU:
                    gates(t - 6)
                if 0 <= t - 2 < NU:
                    logits(t - 2)
                if 0 <= t - 1 < NU:
                    norm_transposes(t - 1)
                if 0 <= t - 5 < NU:
                    norm2_transposes(t - 5)
                if 0 <= t - 3 < NU:
                    probs_transposes(t - 3)

            pe.wait_ge(onehot_ready, 1)
            pe.wait_ge(consts, 8)
            te.matmul(bank[6][:], before[:], onehot[:].rearrange("p i e -> p (i e)"), start=True, stop=True)
            te.matmul(bank[7][:], ones_bf[:], onehot[:].rearrange("p i e -> p (i e)"), start=True, stop=True).then_inc(ranks_ready, 1)
            pe.wait_ge(shared_in, 48)
            with pe.Fori(0, NG // 2) as it:
                def shared_up(g2, m):
                    n = KF * g2 + m
                    pe.wait_ge(sh_h, 2 * KF * it + n - 2 + 1 + FREE2)
                    tok = bass.ds((2 * it + g2) * GT, GT)
                    for w, b in ((shg, 0), (shu, 2)):
                        for k in range(KD):
                            ins = te.matmul(bank[b + n % 2][:], w[:, k, m * P:(m + 1) * P], xnT[:, k, tok],
                                            start=(k == 0), stop=(k == KD - 1))
                    ins.then_inc(sh_gu, 1)

                def shared_down(g2):
                    pe.wait_ge(sh_h, 2 * KF * it + KF * (g2 + 1) + FREE2)
                    for w in (2 * g2, 2 * g2 + 1):
                        if w >= 2:
                            pe.wait_ge(residual_ready, 4 * it + w - 1)
                        else:
                            pe.wait_ge(residual_ready, 4 * it)
                        for j in (0, 1):
                            c = (2 * (w - 2 * g2) + j) * P
                            for m in range(KF):
                                ins = te.matmul(bank[4 + w % 2][:, j * D:(j + 1) * D], h_s[:, g2, m, c:c + P],
                                                shd[:, m], start=(m == 0), stop=(m == KF - 1))
                        ins.then_inc(sh_down, 1)

                for m in range(KF):
                    shared_up(0, m)
                shared_up(1, 0)
                shared_up(1, 1)
                shared_down(0)
                shared_up(1, 2)
                shared_up(1, 3)
                shared_down(1)

            pe.wait_ge(residual_ready, NU)
            pe.wait_ge(slot_ready, 2)
            te.matmul(bank[0][0:1, 0:P], begin_f[:], ident[:], start=True, stop=True).then_inc(begin_done, 1)

            for u in range(NU):
                b = u % SORTED_RING
                pe.wait_ge(sorted_in[b], 16 * (u // SORTED_RING + 1))
                if u >= 2:
                    pe.wait_ge(xsT_ready, u)
                transpose_pair(bank[6 + u % 2], sorted_pair[b], 0, tX)

            def gate_up(c, s):
                pe.wait_ge(x_ready, c + 1)
                pe.wait_ge(h_ready, c)
                for w, done in ((0, g_done), (1, u_done)):
                    for k in range(KD):
                        for a in range(HALVES):
                            ins = te.matmul(bank[w][a * LW:(a + 1) * LW, 0:FH], x_c[:, k],
                                            ring_gu[:, s, w, k, a * FH:(a + 1) * FH],
                                            start=(k == 0), stop=(k == KD - 1))
                            if k == KD - 1:
                                ins.then_inc(done, 1)

            def down_of(n, s):
                pe.wait_ge(hT_ready, n)
                pe.wait_ge(y_ready, n)
                for m in range(KF):
                    mh, mp = m // (KF // HALVES), m % (KF // HALVES)
                    for a in range(HALVES):
                        ins = te.matmul(bank[4][a * LW:(a + 1) * LW, 0:DH], hT[:, mp, mh * LW:(mh + 1) * LW],
                                        ring_d[:, s, m, a * DH:(a + 1) * DH],
                                        start=(m == 0), stop=(m == KF - 1))
                        if m == KF - 1:
                            ins.then_inc(down_done, 1)

            def h_transposes(c):
                pe.wait_ge(h_ready, c + 1)
                pe.wait_ge(hT_ready, c)
                for m in range(KF // HALVES):
                    ins = te.transpose(bank[3][:, m * P:(m + 1) * P], h_r[:, m * P:(m + 1) * P], ident[:])
                ins.then_inc(hT_done, 1)

            pe.wait_ge(table_ready, 3)
            with pe.Fori(0, NE // RING) as it:
                for s in range(RING):
                    e = RING * it + s
                    c0 = pe.value_load(chunk_first[0:1, bass.ds(e, 1)], min_val=0, max_val=MAX_CHUNKS - 1)
                    n = pe.value_load(chunk_n[0:1, bass.ds(e, 1)], min_val=1, max_val=MAX_CHUNKS - NE + 1)
                    pe.wait_ge(gu_in[s], 32 * it + 32)
                    gate_up(c0, s)
                    if s:
                        down_of(c0, s - 1)
                    else:
                        with pe.If(it > 0):
                            down_of(c0, RING - 1)
                    h_transposes(c0)
                    pe.wait_ge(d_in[s], 16 * it + 16)
                    with pe.If(n > 1):
                        with pe.Fori(1, n) as j:
                            gate_up(c0 + j, s)
                            down_of(c0 + j, s)
                            h_transposes(c0 + j)
                        pe.nop()
            pairs = pair_count(pe)
            odd = pe.value_load(pair_n[0:1, 1:2], min_val=0, max_val=1)
            with pe.If(odd > 0):
                end = pe.value_load(chunk_end[0:1, NE - 1:NE], min_val=NE, max_val=MAX_CHUNKS)
                gate_up(end, RING - 1)
                down_of(end, RING - 1)
                h_transposes(end)
            down_of(2 * pairs, RING - 1)
    return nc


_INS = ["x", "ctx_1024", "mask_1xSxS2_ff0", "L0_xattn_kernel_q", "L0_xattn_bias_q", "L0_xattn_kernel_k",
        "L0_xattn_bias_k", "L0_xattn_kernel_v", "L0_xattn_bias_v", "L0_ffn_gate_w",
        "L0_ffn_shared_gate_w", "L0_ffn_shared_up_w", "L0_ffn_shared_down_w",
        "L0_ffn_routed_gate_w", "L0_ffn_routed_up_w", "L0_ffn_routed_down_w"]


def kernel(**inputs):
    import numpy as _np
    import concourse.bacc as _bacc
    from concourse import mybir as _mybir
    from concourse.bass_utils import run_bass_kernel_spmd as _run

    nc = _bacc.Bacc("TRN2", target_bir_lowering=False, num_devices=1)
    arrays, args = {}, []
    for name in _INS:
        a = _np.ascontiguousarray(inputs[name])
        arrays[f"in_{name}_dram"] = a
        args.append(nc.dram_tensor(f"in_{name}_dram", a.shape, _mybir.dt.from_np(a.dtype), kind="ExternalInput").ap())
    shape = inputs["x"].shape
    args.append(nc.dram_tensor("out_0_dram", shape, _mybir.dt.float32, kind="ExternalOutput").ap())
    build_cross_attention_moe(nc, *args)
    r = _run(nc, [arrays], core_ids=[0])
    return r.results[0]["out_0_dram"]
```

```python
from contextlib import ExitStack

import concourse.bass as bass
from concourse import mybir

ALU = mybir.AluOpType
ACT = mybir.ActivationFunctionType
AX = mybir.AxisListType
F32 = mybir.dt.float32
BF16 = mybir.dt.bfloat16
I32 = mybir.dt.int32
U32 = mybir.dt.uint32
P = 128


def build_cross_attention_moe(nc, x, ctx_in, mask, wq, bq, wk, bk, wv, bv, gate_w,
                              sh_gate_w, sh_up_w, sh_down_w, ex_gate_w, ex_up_w, ex_down_w, out):
    B, S, D = x.shape
    KV = ctx_in.shape[1]
    NE = gate_w.shape[1]
    FF = sh_gate_w.shape[1]
    T = B * S
    NT = T // P
    NTB = S // P
    NU = NT // 2
    KD = D // P
    KF = FF // P
    GT = 512
    HALVES = 2
    LW = P // HALVES
    MAX_CHUNKS = NE + (T - NE) // LW
    MAX_PAIRS = (MAX_CHUNKS + 1) // 2
    FH, DH = FF // HALVES, D // HALVES
    RING = 8
    SORTED_RING = 4
    EPS = 1e-5
    SCALE = float(D) ** -0.5
    LOG_LW = LW.bit_length() - 1
    assert D == 256 and KD == 2 and GT == 4 * P and NE % RING == 0 and FF == 512
    assert 2 * MAX_PAIRS < P

    x_t = x.rearrange("b s d -> (b s) d").rearrange("(i p) d -> p i d", p=P)
    out_t = out.rearrange("b s d -> (b s) d").rearrange("(i p) d -> p i d", p=P)
    sorted_rows = nc.dram_tensor("sorted_rows", [T, D], F32, kind="Internal").ap()
    sorted_t = sorted_rows.rearrange("(i p) d -> p i d", p=P)
    slot_rows = nc.dram_tensor("slot_rows", [2 * MAX_PAIRS * LW, D], F32, kind="Internal").ap()
    slot_c = slot_rows.rearrange("(c t) (a d) -> c a t d", t=LW, a=HALVES)

    with ExitStack() as st:
        def sb(name, shape, dt=F32):
            return st.enter_context(nc.sbuf_tensor(name, shape, dt))

        def sem(name):
            return st.enter_context(nc.semaphore(name))

        bank = [st.enter_context(nc.psum_tensor(f"bank{i}", [P, 512], F32)) for i in range(8)]

        ident = sb("ident", [P, P])
        before = sb("before", [P, P], BF16)
        ones_bf = sb("ones_bf", [P, P], BF16)
        ones_row = sb("ones_row", [1, 2 * P])
        ones_scan = sb("ones_scan", [P, NE * NT])
        iota_row = sb("iota_row", [P, P])
        iota_p = sb("iota_p", [P, 1])
        power = sb("power", [P, NT])
        zeros = sb("zeros", [P, 1, D])
        h_place = sb("h_place", [P, 2 * KF * GT])
        taken = [0]

        def carve(parts, *shape):
            n = 1
            for s_ in shape:
                n *= s_
            a = taken[0]
            taken[0] += n
            assert taken[0] <= 2 * KF * GT
            view = h_place[0:parts, a:a + n]
            if len(shape) == 2:
                view = view.rearrange("p (a b) -> p a b", a=shape[0])
            return view

        h_s = h_place[:].rearrange("p (g m t) -> p g m t", g=2, m=KF)
        wq_sb = carve(P, KD, D)
        wk_sb = carve(P, KD, D)
        wv_sb = carve(P, KD, D)
        ctx_sb = carve(KV, B, D)
        ctxT = carve(P, KD, B * KV)
        wqT = carve(P, KD, D)
        kT = carve(P, KD, B * KV)
        bq_wide = carve(P, KD, P)
        mask_sb = carve(P, NTB, KV)
        bq_row = sb("bq_row", [1, D])
        bk_row = sb("bk_row", [1, D])
        bv_row = sb("bv_row", [1, D])
        v_sb = sb("v_sb", [KV, B, D])
        qk = sb("qk", [P, KD, B * KV])
        bias_k = sb("bias_k", [P, B * KV])
        mask_b = sb("mask_b", [P, B, NTB, KV])
        x1 = sb("x1", [P, NT, D])
        xs_flat = sb("xs_flat", [P, KD * (T + LW)])
        xn = xs_flat[:, 0:NT * D].rearrange("p (i d) -> p i d", i=NT)
        xsT = xs_flat[:].rearrange("p (k t) -> p k t", k=KD)
        pairT = sb("pairT", [P, 2, 2, KD, P])
        tot_first = pairT[:].rearrange("p a b c d -> p (a b c d)").rearrange("p (w e i) -> p w e i", w=2, e=NE)
        tot, first = tot_first[:, 0], tot_first[:, 1]
        probs = sb("probs", [P, 6, KV])
        pT = sb("pT", [KV, 2, 2, P])
        stats1 = sb("stats1", [P, NT, 6])
        stats2 = sb("stats2", [P, NT, 6])
        mv1 = sb("mv1", [P, NT, 2])
        mv2 = sb("mv2", [P, NT, 2])
        var1 = sb("var1", [P, NT])
        var2 = sb("var2", [P, NT])
        rstd1 = sb("rstd1", [P, NT])
        shift1 = sb("shift1", [P, NT])
        rstd2 = sb("rstd2", [P, NT])
        nmax = sb("nmax", [P, NT])
        psum_p = sb("psum_p", [P, NT])
        rsum = sb("rsum", [P, NT])
        xnT = sb("xnT", [P, KD, T])
        gate_sb = sb("gate_sb", [P, KD, NE])
        top8 = sb("top8", [P, NT, 8])
        idx8 = sb("idx8", [P, NT, 8], U32)
        half_tanh = sb("half_tanh", [P, NT])
        score = sb("score", [P, NT])
        expert_f = sb("expert_f", [P, NT])
        onehot = sb("onehot", [P, NT, NE], BF16)
        place = mask_b[:].rearrange("p b i k -> p (b i k)")[:, 0:NT * NE].rearrange("p (i e) -> p i e", i=NT)
        pos_f = sb("pos_f", [P, NT])
        pos = sb("pos", [P, NT], I32)
        count_f = sb("count_f", [P, NE])
        chunk_i = sb("chunk_i", [P, NE], I32)
        chunk_f = sb("chunk_f", [P, NE])
        chunk_cum = sb("chunk_cum", [P, NE])
        adjust = sb("adjust", [P, NE])
        padding = sb("padding", [P, NE])
        slot_f = sb("slot_f", [P, NT])
        slot_i = sb("slot_i", [P, NT], I32)
        done_before = sb("done_before", [P, NE])
        begin_f = sb("begin_f", [P, 1])
        begin = sb("begin", [1, P], I32)
        chunk_first = sb("chunk_first", [1, NE], I32)
        pair_f = sb("pair_f", [1, 3])
        pair_n = sb("pair_n", [1, 3], I32)
        chunk_end = sb("chunk_end", [1, NE], I32)
        shg = sb("shg", [P, KD, FF])
        shu = sb("shu", [P, KD, FF])
        shd = sb("shd", [P, KF, D])
        ring_gu = sb("ring_gu", [P, RING, 2, KD, FF])
        ring_d = sb("ring_d", [P, RING, KF, D])
        taken[0] = 0
        x_c = carve(P, KD, LW)
        h_r = carve(P, FH)
        hT = carve(P, KF // HALVES, P)
        y_c = carve(P, 2, DH)
        y_t = xn
        sorted_own = sb("sorted_own", [P, 4, D])
        sorted_pair = [sorted_own[:, 0:2], sorted_own[:, 2:4]] + [
            pairT[:, b].rearrange("p j k c -> p (j k c)").rearrange("p (t d) -> p t d", t=2) for b in (0, 1)]

        x_in = [sem(f"x_in{g}") for g in range(4)]
        ctx_q_in = sem("ctx_q_in")
        k_bias_in = sem("k_bias_in")
        v_in = sem("v_in")
        mask_in = sem("mask_in")
        gate_in = sem("gate_in")
        shared_in = sem("shared_in")
        gu_in = [sem(f"gu_in{s}") for s in range(RING)]
        d_in = [sem(f"d_in{s}") for s in range(RING)]
        zeros_out = sem("zeros_out")
        scattered = sem("scattered")
        sorted_in = [sem(f"sorted_in{g}") for g in range(SORTED_RING)]
        y_stored = [sem(f"y_stored{q}") for q in (0, 1)]
        y_in = [sem(f"y_in{u}") for u in range(NU)]
        out_done = sem("out_done")
        pool_step = sem("pool_step")
        dve_step = sem("dve_step")
        consts = sem("consts")
        prep_pe = sem("prep_pe")
        prep_act = sem("prep_act")
        prep_dve = sem("prep_dve")
        ln1_stats = sem("ln1_stats")
        rstd1_ready = sem("rstd1_ready")
        xn_ready = sem("xn_ready")
        normT_done = sem("normT_done")
        pairT_ready = sem("pairT_ready")
        logits_ready = sem("logits_ready")
        scores_ready = sem("scores_ready")
        probs_ready = sem("probs_ready")
        probsT_done = sem("probsT_done")
        pT_ready = sem("pT_ready")
        av_ready = sem("av_ready")
        x1_ready = sem("x1_ready")
        ln2_stats = sem("ln2_stats")
        rstd2_ready = sem("rstd2_ready")
        xn2_ready = sem("xn2_ready")
        norm2T_done = sem("norm2T_done")
        xnT_ready = sem("xnT_ready")
        gate_ready = sem("gate_ready")
        top_ready = sem("top_ready")
        tanh_ready = sem("tanh_ready")
        score_ready = sem("score_ready")
        xs_ready = sem("xs_ready")
        onehot_ready = sem("onehot_ready")
        ranks_ready = sem("ranks_ready")
        pos_ready = sem("pos_ready")
        slot_ready = sem("slot_ready")
        begin_done = sem("begin_done")
        sortedT_done = sem("sortedT_done")
        xsT_ready = sem("xsT_ready")
        table_ready = sem("table_ready")
        sh_gu = sem("sh_gu")
        sh_tanh = sem("sh_tanh")
        sh_h = sem("sh_h")
        sh_down = sem("sh_down")
        residual_ready = sem("residual_ready")
        x_ready = sem("x_ready")
        g_done = sem("g_done")
        u_done = sem("u_done")
        silu_done = sem("silu_done")
        h_ready = sem("h_ready")
        hT_done = sem("hT_done")
        hT_ready = sem("hT_ready")
        down_done = sem("down_done")
        y_ready = sem("y_ready")
        sum_ready = sem("sum_ready")
        pool_waited = sem("pool_waited")

        PARTS = "p (t n) -> p t n"
        FLAT = "p a b -> p (a b)"
        FREE1 = 1
        EARLY_PARTS = {t: t - 7 for t in range(7, NU + 6)}
        LATE = len(EARLY_PARTS)

        def shared_banks(n):
            if n == 3 * KF:
                return bank[4], bank[5]
            return (bank[6], bank[7]) if n < 2 * KF or n % 2 else (bank[2], bank[3])

        def pair_count(eng):
            return eng.value_load(pair_n[0:1, 0:1], min_val=NE // 2, max_val=MAX_PAIRS)

        block = st.enter_context(nc.Block())

        @block.sync
        def _(sp):
            def load_expert(e, s):
                sp.dma_start(ring_gu[:, s, 0], ex_gate_w[bass.ds(e, 1)].rearrange("a (k p) f -> p (a k) f", p=P)).then_inc(gu_in[s], 16)
                sp.dma_start(ring_gu[:, s, 1], ex_up_w[bass.ds(e, 1)].rearrange("a (k p) f -> p (a k) f", p=P)).then_inc(gu_in[s], 16)
                sp.dma_start(ring_d[:, s], ex_down_w[bass.ds(e, 1)].rearrange("a (m p) d -> p (a m) d", p=P)).then_inc(d_in[s], 16)

            def load_rows(dst, src, done):
                sp.dma_start(dst, src.rearrange("(k p) d -> p k d", p=P)).then_inc(done, 16)

            def load_bias(dst, src, done):
                sp.dma_start(dst[:], src.rearrange("(a d) -> a d", a=1)).then_inc(done, 16)

            sp.dma_start(ctx_sb, ctx_in.rearrange("b k d -> k b d")).then_inc(ctx_q_in, 16)
            load_rows(wq_sb, wq, ctx_q_in)
            load_rows(wk_sb, wk, k_bias_in)
            load_bias(bk_row, bk, k_bias_in)
            load_bias(bq_row, bq, k_bias_in)
            sp.dma_start(x1[:, 0:4], x_t[:, 0:4]).then_inc(x_in[0], 16)
            load_rows(wv_sb, wv, v_in)
            load_bias(bv_row, bv, v_in)
            sp.dma_start(mask_sb, mask[0].rearrange("(i p) k -> p i k", p=P)).then_inc(mask_in, 16)
            for g in range(1, 4):
                sp.dma_start(x1[:, 4 * g:4 * g + 4], x_t[:, 4 * g:4 * g + 4]).then_inc(x_in[g], 16)
            sp.dma_start(gate_sb[:], gate_w.rearrange("(k p) e -> p k e", p=P)).then_inc(gate_in, 16)
            sp.dma_start(shg[:], sh_gate_w.rearrange("(k p) f -> p k f", p=P)).then_inc(shared_in, 16)
            sp.dma_start(shu[:], sh_up_w.rearrange("(k p) f -> p k f", p=P)).then_inc(shared_in, 16)
            sp.dma_start(shd[:], sh_down_w.rearrange("(m p) d -> p m d", p=P)).then_inc(shared_in, 16)
            for s in range(RING):
                load_expert(s, s)
            sp.wait_ge(consts, 9)
            sp.dma_start(slot_rows[NE * LW:].rearrange("(p r) d -> p r d", p=P),
                         zeros[:].to_broadcast([P, (2 * MAX_PAIRS - NE) * LW // P, D])).then_inc(zeros_out, 16)
            sp.wait_ge(scattered, 16 * NT)
            sp.wait_ge(slot_ready, 2)
            for u in range(NU):
                b = u % SORTED_RING
                if u >= SORTED_RING:
                    sp.wait_ge(sortedT_done, u - SORTED_RING + 1)
                sp.dma_start(sorted_pair[b], sorted_t[:, 2 * u:2 * u + 2]).then_inc(sorted_in[b], 16)
            sp.wait_ge(table_ready, 2)
            with sp.Fori(0, NE // RING - 1) as it:
                for s in range(RING):
                    e = RING * it + s
                    end = sp.value_load(chunk_end[0:1, bass.ds(e, 1)], min_val=1, max_val=MAX_CHUNKS)
                    sp.wait_ge(down_done, HALVES * end)
                    load_expert(e + RING, s)
            for u in range(NU):
                sp.wait_ge(sum_ready, u + 1)
                sp.dma_start(out_t[:, 2 * u:2 * u + 2], x1[:, 2 * u:2 * u + 2]).then_inc(out_done, 16)
            sp.wait_ge(out_done, 16 * NU)

        @block.gpsimd
        def _(pool):
            steps = [0]

            def step(ins):
                steps[0] += 1
                ins.then_inc(pool_step, 1)
                pool.wait_ge(pool_step, steps[0])

            g_ = nc.gpsimd
            step(g_.memset(ident[:], 0.0))
            g_.affine_select(out=ident[:], in_=ident[:], compare_op=ALU.not_equal, fill=1.0, base=0,
                             pattern=[[-1, P]], channel_multiplier=1).then_inc(consts, 1)
            g_.memset(ones_row[:], 1.0).then_inc(consts, 1)
            g_.memset(power[:], -0.5).then_inc(consts, 1)
            g_.memset(zeros[:], 0.0).then_inc(consts, 1)
            pool.wait_ge(consts, 4)

            def rstd_1(g):
                a = 4 * g
                pool.wait_ge(ln1_stats, 4 * g + 4)
                step(g_.tensor_scalar(var1[:, a:a + 4], mv1[:, a:a + 4, 1], EPS, None, ALU.add))
                step(g_.tensor_tensor(rstd1[:, a:a + 4], var1[:, a:a + 4], power[:, 0:4], ALU.pow))
                step(g_.tensor_tensor(shift1[:, a:a + 4], mv1[:, a:a + 4, 0], rstd1[:, a:a + 4], ALU.mult))
                g_.tensor_scalar(shift1[:, a:a + 4], shift1[:, a:a + 4], -1.0, None, ALU.mult).then_inc(rstd1_ready, 1)

            rstd_1(0)
            rstd_1(1)
            g_.memset(ones_bf[:], 1.0).then_inc(consts, 1)
            step(g_.memset(before[:], 0.0))
            g_.affine_select(out=before[:], in_=before[:], compare_op=ALU.is_ge, fill=1.0, base=0,
                             pattern=[[-1, P]], channel_multiplier=1).then_inc(consts, 1)
            g_.iota(iota_row[:], pattern=[[1, P]], base=0, channel_multiplier=0,
                    allow_small_or_imprecise_dtypes=True).then_inc(consts, 1)
            g_.iota(iota_p[:], pattern=[[0, 1]], base=0, channel_multiplier=1,
                    allow_small_or_imprecise_dtypes=True).then_inc(consts, 1)
            g_.memset(ones_scan[:], 1.0).then_inc(consts, 1)
            rstd_1(2)
            rstd_1(3)

            def rstd_2(u):
                a = 2 * u
                pool.wait_ge(ln2_stats, 2 * u + 2)
                step(g_.tensor_scalar(var2[:, a:a + 2], mv2[:, a:a + 2, 1], EPS, None, ALU.add))
                g_.tensor_tensor(rstd2[:, a:a + 2], var2[:, a:a + 2], power[:, 0:2], ALU.pow).then_inc(rstd2_ready, 1)

            def scores(u):
                a = 2 * u
                pool.wait_ge(tanh_ready, u + 1)
                g_.tensor_scalar(score[:, a:a + 2], half_tanh[:, a:a + 2], 0.5, 0.5, ALU.mult, ALU.add).then_inc(score_ready, 1)

            for t in range(4, NU + 7):
                if 0 <= t - 4 < NU:
                    rstd_2(t - 4)
                if 0 <= t - 7 < NU:
                    scores(t - 7)

            pool.wait_ge(xs_ready, NT)
            pool.wait_ge(pos_ready, 1)
            for i in range(NT):
                g_.indirect_dma_start(
                    out=sorted_rows, out_offset=bass.IndirectOffsetOnAxis(ap=pos[:, i:i + 1], axis=0),
                    in_=xn[:, i, :], in_offset=None).then_inc(scattered, 16)
            pool.wait_ge(scattered, 16 * NT)
            g_.memset(xsT[:, :, T:T + LW], 0.0).then_inc(xsT_ready, 1)

            pool.wait_ge(table_ready, 2)
            pairs = pair_count(pool)
            for q in (0, 1):
                pool.wait_ge(y_stored[q], 16 * pairs)
            pool.sem_inc(pool_waited, 1)
            for i in range(NT):
                g_.indirect_dma_start(
                    out=y_t[:, i, :], out_offset=None, in_=slot_rows,
                    in_offset=bass.IndirectOffsetOnAxis(ap=slot_i[:, i:i + 1], axis=0)).then_inc(y_in[i // 2], 16)

        @block.vector
        def _(dve):
            v = nc.vector
            steps = [0]

            def step(ins):
                steps[0] += 1
                ins.then_inc(dve_step, 1)
                dve.wait_ge(dve_step, steps[0])

            def layer_stats(u, stats, mv, done):
                a = 2 * u
                steps[0] += 1
                v.bn_stats(stats[:, a], x1[:, a]).then_inc(dve_step, 1)
                step(v.bn_stats(stats[:, a + 1], x1[:, a + 1]))
                for i in (a, a + 1):
                    v.bn_aggr(mv[:, i], stats[:, i]).then_inc(done, 1)

            def stage_mask(u):
                a = 2 * u
                dve.wait_ge(logits_ready, u + 1)
                c = 2 * (u % 3)
                if u >= 3:
                    dve.wait_ge(probsT_done, u - 2)
                step(v.tensor_tensor(probs[:, c:c + 2], bank[1][:, 0:2 * KV].rearrange(PARTS, t=2),
                                     mask_b[:, a // NTB, a % NTB:a % NTB + 2], ALU.add))
                v.tensor_reduce(nmax[:, a:a + 2], probs[:, c:c + 2], AX.X, ALU.max, negate=True).then_inc(scores_ready, 1)

            def stage_x1(u):
                a = 2 * u
                dve.wait_ge(probs_ready, 2 * u + 2)
                step(v.reciprocal(rsum[:, a:a + 2], psum_p[:, a:a + 2]))
                dve.wait_ge(av_ready, u + 1)
                dve.wait_ge(xn_ready, 2 * u + 2)
                for j in (0, 1):
                    v.scalar_tensor_tensor(out=x1[:, a + j], in0=bank[3][:, j * D:(j + 1) * D],
                                           scalar=rsum[:, a + j:a + j + 1], in1=x1[:, a + j],
                                           op0=ALU.mult, op1=ALU.add).then_inc(x1_ready, 1)
                dve.wait_ge(x1_ready, 2 * u + 2)
                layer_stats(u, stats2, mv2, ln2_stats)

            def stage_xn2(u):
                a = 2 * u
                dve.wait_ge(rstd2_ready, u + 1)
                dve.wait_ge(normT_done, u + 1)
                for i in (a, a + 1):
                    v.tensor_scalar(xn[:, i], x1[:, i], mv2[:, i, 0:1], rstd2[:, i:i + 1],
                                    ALU.subtract, ALU.mult).then_inc(xn2_ready, 1)

            def stage_top(u):
                a = 2 * u
                dve.wait_ge(gate_ready, u + 1)
                for j in (0, 1):
                    g = bank[5][:, j * NE:(j + 1) * NE]
                    step(v.max(top8[:, a + j], g))
                    v.max_index(idx8[:, a + j], top8[:, a + j], g).then_inc(top_ready, 1)

            def shared_h(n):
                h = h_s[:, n // KF % 2, n % KF]
                g, u = shared_banks(n)
                dve.wait_ge(sh_tanh, n + 1)
                step(v.scalar_tensor_tensor(out=h, in0=h, scalar=1.0, in1=g[:], op0=ALU.add, op1=ALU.mult))
                v.scalar_tensor_tensor(out=h, in0=h, scalar=0.5, in1=u[:], op0=ALU.mult, op1=ALU.mult).then_inc(sh_h, 1)

            def shared_residual(w):
                dve.wait_ge(sh_down, w + 1)
                rows = x1[:, 2 * w:2 * w + 2]
                v.tensor_tensor(rows, bank[4 + w % 2][:].rearrange(PARTS, t=2), rows, ALU.add).then_inc(residual_ready, 1)

            dve.wait_ge(prep_pe, 1)
            v.tensor_copy(ctxT.rearrange("p k n -> p (k n)"), bank[6][:, 0:KD * B * KV]).then_inc(prep_dve, 1)
            for u in (0, 1):
                dve.wait_ge(x_in[0], 16)
                layer_stats(u, stats1, mv1, ln1_stats)
            dve.wait_ge(prep_pe, 4)
            v.tensor_copy(kT.rearrange("p k n -> p (k n)"), bank[5][:, 0:KD * B * KV]).then_inc(prep_dve, 1)
            dve.wait_ge(prep_pe, 5)
            step(v.tensor_scalar(bias_k[:], bank[1][:, 0:B * KV], SCALE, None, ALU.mult))
            dve.wait_ge(mask_in, 16)
            for b in range(B):
                v.tensor_tensor(mask_b[:, b], mask_sb,
                                bias_k[:, b * KV:(b + 1) * KV].rearrange("p (a k) -> p a k", a=1).to_broadcast([P, NTB, KV]),
                                ALU.add).then_inc(prep_dve, 1)
            for u in range(2, 4):
                dve.wait_ge(x_in[u // 2], 16)
                layer_stats(u, stats1, mv1, ln1_stats)
            dve.wait_ge(prep_dve, 4)
            for t in range(2, NU + 7):
                if 0 <= t - 4 < NU:
                    stage_x1(t - 4)
                if 0 <= t - 6 < NU:
                    stage_top(t - 6)
                if 0 <= t - 2 < NU:
                    stage_mask(t - 2)
                if t in (2, 3):
                    for u in (2 * t, 2 * t + 1):
                        dve.wait_ge(x_in[u // 2], 16)
                        layer_stats(u, stats1, mv1, ln1_stats)
                if 0 <= t - 4 < NU:
                    stage_xn2(t - 4)
                if t in EARLY_PARTS and EARLY_PARTS[t] < LATE - 1:
                    shared_h(EARLY_PARTS[t])

            dve.wait_ge(top_ready, NT)
            dve.wait_ge(consts, 9)
            step(v.tensor_copy(expert_f[:], idx8[:, :, 0]))
            v.tensor_tensor(onehot[:], iota_row[:, 0:NE].rearrange("p (a e) -> p a e", a=1).to_broadcast([P, NT, NE]),
                            expert_f[:].rearrange("p (i a) -> p i a", a=1).to_broadcast([P, NT, NE]),
                            ALU.is_equal).then_inc(onehot_ready, 1)
            shared_h(LATE - 1)
            dve.wait_ge(onehot_ready, 1)
            dve.wait_ge(ranks_ready, 1)
            step(v.tensor_copy(tot, bank[1][:].rearrange("p (i e) -> p e i", e=NE)))
            step(v.tensor_tensor_scan(first.rearrange(FLAT), ones_scan[:], tot.rearrange(FLAT), 0.0,
                                      ALU.mult, ALU.add))
            step(v.tensor_tensor(first, first, tot, ALU.subtract))
            step(v.tensor_tensor(place, bank[0][:].rearrange("p (i e) -> p i e", e=NE),
                                 first.rearrange("p e i -> p i e"), ALU.add))
            step(v.tensor_tensor(place, place, onehot[:], ALU.mult))
            step(v.tensor_reduce(pos_f[:], place, AX.X, ALU.add))
            v.tensor_copy(pos[:], pos_f[:]).then_inc(pos_ready, 1)
            step(v.tensor_reduce(count_f[:], tot, AX.X, ALU.add))
            step(v.tensor_scalar(chunk_f[:], count_f[:], 1.0, LW - 1.0, ALU.max, ALU.add))
            step(v.tensor_copy(chunk_i[:], chunk_f[:]))
            step(v.tensor_scalar(chunk_i[:], chunk_i[:], LOG_LW, None, ALU.arith_shift_right))
            step(v.tensor_copy(chunk_f[:], chunk_i[:]))
            steps[0] += 1
            v.tensor_tensor_scan(chunk_cum[:], ones_scan[:, 0:NE], chunk_f[:], 0.0, ALU.mult, ALU.add).then_inc(dve_step, 1)
            step(v.scalar_tensor_tensor(out=padding[:], in0=chunk_f[:], scalar=float(LW), in1=count_f[:],
                                        op0=ALU.mult, op1=ALU.subtract))
            step(v.tensor_tensor_scan(adjust[:], ones_scan[:, 0:NE], padding[:], 0.0, ALU.mult, ALU.add))
            step(v.tensor_tensor(adjust[:], adjust[:], padding[:], ALU.subtract))
            step(v.tensor_tensor(place, onehot[:],
                                 adjust[:].rearrange("p (a e) -> p a e", a=1).to_broadcast([P, NT, NE]), ALU.mult))
            step(v.tensor_reduce(slot_f[:], place, AX.X, ALU.add))
            step(v.tensor_tensor(slot_f[:], slot_f[:], pos_f[:], ALU.add))
            v.tensor_copy(slot_i[:], slot_f[:]).then_inc(slot_ready, 1)
            step(v.tensor_scalar(done_before[:], chunk_cum[:], iota_p[:], None, ALU.is_le))
            step(v.tensor_tensor(done_before[:], done_before[:], padding[:], ALU.mult))
            step(v.tensor_reduce(begin_f[:], done_before[:], AX.X, ALU.add))
            v.scalar_tensor_tensor(out=begin_f[:], in0=iota_p[:], scalar=float(LW), in1=begin_f[:],
                                   op0=ALU.mult, op1=ALU.subtract).then_inc(slot_ready, 1)
            step(v.tensor_scalar(pair_f[:, 0:1], chunk_cum[0:1, NE - 1:NE], 1.0, None, ALU.add))
            step(v.tensor_copy(pair_n[:, 0:1], pair_f[:, 0:1]))
            step(v.tensor_scalar(pair_n[:, 0:1], pair_n[:, 0:1], 1, None, ALU.arith_shift_right))
            step(v.tensor_copy(pair_f[:, 0:1], pair_n[:, 0:1]))
            step(v.scalar_tensor_tensor(out=pair_f[:, 1:2], in0=pair_f[:, 0:1], scalar=2.0, in1=chunk_cum[0:1, NE - 1:NE],
                                        op0=ALU.mult, op1=ALU.subtract))
            step(v.tensor_scalar(pair_f[:, 2:3], pair_f[:, 0:1], -1.0, None, ALU.add))
            step(v.tensor_copy(pair_n[:, 1:3], pair_f[:, 1:3]))
            v.tensor_copy(chunk_end[:], chunk_cum[0:1]).then_inc(table_ready, 1)
            v.tensor_tensor(chunk_first[:], chunk_cum[0:1], chunk_f[0:1], ALU.subtract).then_inc(table_ready, 1)

            shared_residual(0)
            shared_residual(1)
            for n in range(LATE, 3 * KF):
                shared_h(n)
            for w in range(2, NU - 2):
                shared_residual(w)

            dve.wait_ge(begin_done, 1)
            step(v.tensor_scalar(begin[:], bank[1][0:1, 0:P], float(T), None, ALU.min))

            def take_x(c):
                col = dve.value_load(begin[0:1, bass.ds(c, 1)], min_val=0, max_val=T)
                dve.wait_ge(u_done, HALVES * c)
                v.tensor_copy(x_c, xsT[:, :, bass.ds(col, LW)]).then_inc(x_ready, 1)

            def gated(c):
                dve.wait_ge(silu_done, c + 1)
                dve.wait_ge(u_done, HALVES * (c + 1))
                v.tensor_tensor(h_r, h_r, bank[1][:, 0:FH], ALU.mult).then_inc(h_ready, 1)

            def take_y(c, q, n_stored):
                dve.wait_ge(down_done, HALVES * (c + 1))
                if n_stored is not None:
                    dve.wait_ge(y_stored[q], 16 * n_stored)
                v.tensor_copy(y_c[:, q], bank[4][:, 0:DH]).then_inc(y_ready, 1)

            pairs = pair_count(dve)
            pairs_before = dve.value_load(pair_n[0:1, 2:3], min_val=NE // 2 - 1, max_val=MAX_PAIRS - 1)
            dve.wait_ge(xsT_ready, NU + 1)
            take_x(0)
            shared_h(3 * KF)
            take_x(1)
            gated(0)
            take_x(2)
            gated(1)
            take_y(0, 0, None)
            with dve.Fori(1, pairs) as p:
                take_x(2 * p + 1)
                gated(2 * p)
                take_y(2 * p - 1, 1, p - 1)
                take_x(2 * p + 2)
                gated(2 * p + 1)
                take_y(2 * p, 0, p)
            dve.wait_ge(down_done, HALVES * 2 * pairs)
            dve.wait_ge(y_stored[1], 16 * pairs_before)
            v.tensor_copy(y_c[:, 1], bank[4][:, 0:DH]).then_inc(y_ready, 1)
            for n in range(3 * KF + 1, 4 * KF):
                shared_h(n)
            for u in range(NU):
                if u >= NU - 2:
                    shared_residual(u)
                    dve.wait_ge(residual_ready, u + 1)
                dve.wait_ge(y_in[u], 32)
                v.tensor_tensor(x1[:, 2 * u:2 * u + 2], x1[:, 2 * u:2 * u + 2], y_t[:, 2 * u:2 * u + 2], ALU.add).then_inc(sum_ready, 1)

        @block.scalar
        def _(act):
            a_ = nc.scalar

            act.wait_ge(prep_pe, 2)
            a_.copy(wqT.rearrange("p k n -> p (k n)"), bank[7][:]).then_inc(prep_act, 1)
            act.wait_ge(prep_pe, 3)
            a_.copy(bq_wide.rearrange("p k n -> p (k n)"), bank[4][:, 0:KD * P]).then_inc(prep_act, 1)

            def normalise(u):
                act.wait_ge(rstd1_ready, u // 2 + 1)
                for i in (0, 1):
                    n = 2 * u + i
                    a_.activation(xn[:, n], x1[:, n], ACT.Identity, bias=shift1[:, n:n + 1],
                                  scale=rstd1[:, n:n + 1]).then_inc(xn_ready, 1)

            def keep_normT(u):
                act.wait_ge(normT_done, u + 1)
                if u >= 2:
                    act.wait_ge(logits_ready, u - 1)
                a_.copy(pairT[:, u % 2].rearrange("p j k c -> p (j k c)"), bank[0][:]).then_inc(pairT_ready, 1)

            def exponentials(u):
                act.wait_ge(scores_ready, u + 1)
                for i in (2 * u, 2 * u + 1):
                    p_i = probs[:, 2 * (u % 3) + i % 2]
                    a_.activation(p_i, p_i, ACT.Exp, bias=nmax[:, i:i + 1],
                                  accum_out=psum_p[:, i:i + 1]).then_inc(probs_ready, 1)

            def keep_probsT(u):
                act.wait_ge(probsT_done, u + 1)
                if u >= 2:
                    act.wait_ge(av_ready, u - 1)
                a_.copy(pT[:, u % 2].rearrange("p j c -> p (j c)"), bank[2][0:KV, 0:2 * P]).then_inc(pT_ready, 1)

            def keep_norm2T(u):
                act.wait_ge(norm2T_done, u + 1)
                a_.copy(xnT[:, :, 2 * P * u:2 * P * (u + 1)].rearrange("p k (j c) -> p j k c", j=2),
                        bank[4][:].rearrange("p (j k c) -> p j k c", j=2, k=KD)).then_inc(xnT_ready, 1)

            def top_tanh(u):
                act.wait_ge(top_ready, 2 * u + 2)
                a_.activation(half_tanh[:, 2 * u:2 * u + 2], top8[:, 2 * u:2 * u + 2, 0], ACT.Tanh,
                              scale=0.5).then_inc(tanh_ready, 1)

            act.wait_ge(prep_pe, 6)
            a_.mul(qk[:].rearrange("p k n -> p (k n)"), bank[2][:, 0:KD * B * KV], SCALE).then_inc(prep_act, 1)
            normalise(0)
            act.wait_ge(prep_pe, 7)
            a_.copy(v_sb[:].rearrange("p k n -> p (k n)"), bank[3][0:KV, 0:B * D]).then_inc(prep_act, 1)

            def scaled(u):
                act.wait_ge(score_ready, u + 1)
                act.wait_ge(norm2T_done, u + 1)
                for n in (2 * u, 2 * u + 1):
                    a_.activation(xn[:, n], xn[:, n], ACT.Copy, scale=score[:, n:n + 1]).then_inc(xs_ready, 1)

            def shared_tanh(n):
                act.wait_ge(sh_gu, n + 1)
                if n % KF == 0 and n >= 2 * KF:
                    act.wait_ge(sh_down, 2 * (n // KF - 2) + 2)
                a_.activation(h_s[:, n // KF % 2, n % KF], shared_banks(n)[0][:], ACT.Tanh, scale=0.5).then_inc(sh_tanh, 1)

            for t in range(1, NU + 8):
                if 0 <= t - 3 < NU:
                    exponentials(t - 3)
                if 0 <= t - 5 < NU:
                    keep_norm2T(t - 5)
                if 0 <= t - 3 < NU:
                    keep_probsT(t - 3)
                if 0 <= t - 1 < NU:
                    keep_normT(t - 1)
                if t < NU:
                    normalise(t)
                if 0 <= t - 8 < NU:
                    scaled(t - 8)
                if 0 <= t - 7 < NU:
                    top_tanh(t - 7)
                if t in EARLY_PARTS:
                    shared_tanh(EARLY_PARTS[t])

            for n in range(LATE, 3 * KF):
                shared_tanh(n)

            act.wait_ge(xsT_ready, 1)
            for u in range(NU):
                act.wait_ge(sortedT_done, u + 1)
                a_.copy(xsT[:, :, 2 * P * u:2 * P * (u + 1)].rearrange("p k (j c) -> p j k c", j=2),
                        bank[6 + u % 2][:].rearrange("p (j k c) -> p j k c", j=2, k=KD)).then_inc(xsT_ready, 1)

            def silu(c):
                act.wait_ge(g_done, HALVES * (c + 1))
                act.wait_ge(hT_done, c)
                a_.activation(h_r, bank[0][:, 0:FH], ACT.Silu).then_inc(silu_done, 1)

            def keep_hT(c):
                act.wait_ge(hT_done, c + 1)
                act.wait_ge(down_done, HALVES * c)
                a_.copy(hT.rearrange(FLAT), bank[3][:, 0:FH]).then_inc(hT_ready, 1)

            def store_y(c, q):
                act.wait_ge(y_ready, c + 1 + FREE1)
                act.dma_start(slot_c[bass.ds(c, 1)].rearrange("c a t d -> (c a) t d"), y_c[:, q]).then_inc(y_stored[q], 16)

            act.wait_ge(table_ready, 2)
            pairs = pair_count(act)
            shared_tanh(3 * KF)
            silu(0)
            keep_hT(0)
            silu(1)
            keep_hT(1)
            act.wait_ge(zeros_out, 16)
            store_y(0, 0)
            with act.Fori(1, pairs) as p:
                silu(2 * p)
                keep_hT(2 * p)
                store_y(2 * p - 1, 1)
                silu(2 * p + 1)
                keep_hT(2 * p + 1)
                store_y(2 * p, 0)
            last = pairs * 2 - 1
            act.wait_ge(y_ready, 2 * pairs + FREE1)
            act.dma_start(slot_c[bass.ds(last, 1)].rearrange("c a t d -> (c a) t d"), y_c[:, 1]).then_inc(y_stored[1], 16)
            for n in range(3 * KF + 1, 4 * KF):
                shared_tanh(n)

        @block.tensor
        def _(pe):
            te = nc.tensor
            pe.sem_inc(y_ready, FREE1)

            pe.wait_ge(consts, 3)
            pe.wait_ge(ctx_q_in, 16 * 2)
            for k in range(KD):
                for b in range(B):
                    c = (k * B + b) * KV
                    ins = te.transpose(bank[6][:, c:c + KV], ctx_sb[:, b, k * P:(k + 1) * P], ident[0:KV, 0:KV])
            ins.then_inc(prep_pe, 1)
            for dk in range(KD):
                for ik in range(KD):
                    ins = te.transpose(bank[7][:, dk * D + ik * P:dk * D + (ik + 1) * P],
                                       wq_sb[:, ik, dk * P:(dk + 1) * P], ident[:])
            ins.then_inc(prep_pe, 1)
            pe.wait_ge(k_bias_in, 16 * 3)
            for dk in range(KD):
                ins = te.matmul(bank[4][:, dk * P:(dk + 1) * P], bq_row[:, dk * P:(dk + 1) * P],
                                ones_row[:, 0:P], start=True, stop=True)
            ins.then_inc(prep_pe, 1)
            pe.wait_ge(prep_dve, 1)
            for dk in range(KD):
                o = bank[5][:, dk * B * KV:(dk + 1) * B * KV]
                for ik in range(KD):
                    te.matmul(o, wk_sb[:, ik, dk * P:(dk + 1) * P], ctxT[:, ik], start=(ik == 0), stop=False)
                ins = te.matmul(o, bk_row[:, dk * P:(dk + 1) * P], ones_row[:, 0:B * KV], start=False, stop=True)
            ins.then_inc(prep_pe, 1)
            pe.wait_ge(prep_dve, 2)
            pe.wait_ge(prep_act, 2)
            for dk in range(KD):
                ins = te.matmul(bank[1][:, 0:B * KV], bq_wide[:, dk], kT[:, dk], start=(dk == 0), stop=(dk == KD - 1))
            ins.then_inc(prep_pe, 1)
            for ik in range(KD):
                for dk in range(KD):
                    ins = te.matmul(bank[2][:, ik * B * KV:(ik + 1) * B * KV], wqT[:, dk, ik * P:(ik + 1) * P],
                                    kT[:, dk], start=(dk == 0), stop=(dk == KD - 1))
            ins.then_inc(prep_pe, 1)

            pe.wait_ge(v_in, 16 * 2)
            for b in range(B):
                o = bank[3][0:KV, b * D:(b + 1) * D]
                for ik in range(KD):
                    te.matmul(o, ctxT[:, ik, b * KV:(b + 1) * KV], wv_sb[:, ik], start=(ik == 0), stop=False)
                ins = te.matmul(o, ones_row[:, 0:KV], bv_row[:], start=False, stop=True)
            ins.then_inc(prep_pe, 1)

            def transpose_pair(dst, src, a, done):
                for j in (0, 1):
                    for k in range(KD):
                        c = (j * KD + k) * P
                        ins = te.transpose(dst[:, c:c + P], src[:, a + j, k * P:(k + 1) * P], ident[:])
                ins.then_inc(done, 1)

            def norm_transposes(u):
                pe.wait_ge(xn_ready, 2 * u + 2)
                if u:
                    pe.wait_ge(pairT_ready, u)
                transpose_pair(bank[0], xn, 2 * u, normT_done)

            def logits(u):
                pe.wait_ge(pairT_ready, u + 1)
                if u:
                    pe.wait_ge(scores_ready, u)
                b = 2 * u // NTB
                for j in (0, 1):
                    for k in range(KD):
                        ins = te.matmul(bank[1][:, j * KV:(j + 1) * KV], pairT[:, u % 2, j, k],
                                        qk[:, k, b * KV:(b + 1) * KV], start=(k == 0), stop=(k == KD - 1))
                ins.then_inc(logits_ready, 1)

            def probs_transposes(u):
                pe.wait_ge(probs_ready, 2 * u + 2)
                if u:
                    pe.wait_ge(pT_ready, u)
                for j in (0, 1):
                    ins = te.transpose(bank[2][0:KV, j * P:(j + 1) * P], probs[:, 2 * (u % 3) + j], ident[:])
                ins.then_inc(probsT_done, 1)

            def attend(u):
                pe.wait_ge(pT_ready, u + 1)
                if u:
                    pe.wait_ge(x1_ready, 2 * u)
                for j in (0, 1):
                    ins = te.matmul(bank[3][:, j * D:(j + 1) * D], pT[:, u % 2, j], v_sb[:, 2 * u // NTB],
                                    start=True, stop=True)
                ins.then_inc(av_ready, 1)

            def norm2_transposes(u):
                pe.wait_ge(xn2_ready, 2 * u + 2)
                if u:
                    pe.wait_ge(xnT_ready, u)
                transpose_pair(bank[4], xn, 2 * u, norm2T_done)

            def gates(u):
                pe.wait_ge(xnT_ready, u + 1)
                if u:
                    pe.wait_ge(top_ready, 2 * u)
                for j in (0, 1):
                    for k in range(KD):
                        ins = te.matmul(bank[5][:, j * NE:(j + 1) * NE], xnT[:, k, (2 * u + j) * P:(2 * u + j + 1) * P],
                                        gate_sb[:, k], start=(k == 0), stop=(k == KD - 1))
                ins.then_inc(gate_ready, 1)

            pe.wait_ge(prep_act, 4)
            pe.wait_ge(prep_dve, 4)
            def shared_up(n):
                g, m = n // KF, n % KF
                if 1 <= n < 2 * KF:
                    pe.wait_ge(sh_h, n)
                elif n > 2 * KF:
                    pe.wait_ge(sh_h, n - 1)
                pe.wait_ge(xnT_ready, 2 * g + 2)
                for w, dst in zip((shg, shu), shared_banks(n)):
                    for k in range(KD):
                        ins = te.matmul(dst[:], w[:, k, m * P:(m + 1) * P], xnT[:, k, g * GT:(g + 1) * GT],
                                        start=(k == 0), stop=(k == KD - 1))
                ins.then_inc(sh_gu, 1)

            def shared_down(w):
                pe.wait_ge(sh_h, KF * (w // 2 + 1))
                if w >= 2:
                    pe.wait_ge(residual_ready, w - 1)
                for j in (0, 1):
                    c = (2 * (w % 2) + j) * P
                    for m in range(KF):
                        ins = te.matmul(bank[4 + w % 2][:, j * D:(j + 1) * D], h_s[:, w // 2 % 2, m, c:c + P],
                                        shd[:, m], start=(m == 0), stop=(m == KF - 1))
                ins.then_inc(sh_down, 1)

            for t in range(1, NU + 7):
                if 0 <= t - 4 < NU:
                    attend(t - 4)
                if t == min(EARLY_PARTS):
                    pe.wait_ge(shared_in, 48)
                if 0 <= t - 5 < NU:
                    norm2_transposes(t - 5)
                if 0 <= t - 2 < NU:
                    logits(t - 2)
                if t == 6:
                    pe.wait_ge(gate_in, 16)
                if 0 <= t - 6 < NU:
                    gates(t - 6)
                if 0 <= t - 3 < NU:
                    probs_transposes(t - 3)
                if 0 <= t - 1 < NU:
                    norm_transposes(t - 1)
                if t in EARLY_PARTS:
                    shared_up(EARLY_PARTS[t])

            pe.wait_ge(onehot_ready, 1)
            pe.wait_ge(consts, 9)
            te.matmul(bank[0][:], before[:], onehot[:].rearrange("p i e -> p (i e)"), start=True, stop=True)
            te.matmul(bank[1][:], ones_bf[:], onehot[:].rearrange("p i e -> p (i e)"), start=True, stop=True).then_inc(ranks_ready, 1)

            shared_down(0)
            shared_down(1)
            for n in range(LATE, 3 * KF):
                shared_up(n)
            shared_down(2)
            shared_down(3)
            shared_down(4)

            def sorted_transposes(u):
                b = u % SORTED_RING
                pe.wait_ge(sorted_in[b], 16 * (u // SORTED_RING + 1))
                if u >= 2:
                    pe.wait_ge(xsT_ready, u)
                transpose_pair(bank[6 + u % 2], sorted_pair[b], 0, sortedT_done)

            for u in range(SORTED_RING):
                sorted_transposes(u)
            shared_down(5)
            pe.wait_ge(slot_ready, 2)
            te.matmul(bank[1][0:1, 0:P], begin_f[:], ident[:], start=True, stop=True).then_inc(begin_done, 1)
            for u in range(SORTED_RING, NU):
                sorted_transposes(u)
            pe.wait_ge(residual_ready, NU - 2)
            shared_up(3 * KF)

            def gate_up(c, s):
                pe.wait_ge(x_ready, c + 1)
                for w, done in ((0, g_done), (1, u_done)):
                    for k in range(KD):
                        for a in range(HALVES):
                            ins = te.matmul(bank[w][a * LW:(a + 1) * LW, 0:FH], x_c[:, k],
                                            ring_gu[:, s, w, k, a * FH:(a + 1) * FH],
                                            start=(k == 0), stop=(k == KD - 1))
                            if k == KD - 1:
                                ins.then_inc(done, 1)

            def down_of(n, s):
                pe.wait_ge(hT_ready, n)
                pe.wait_ge(y_ready, n)
                for m in range(KF):
                    mh, mp = m // (KF // HALVES), m % (KF // HALVES)
                    for a in range(HALVES):
                        ins = te.matmul(bank[4][a * LW:(a + 1) * LW, 0:DH], hT[:, mp, mh * LW:(mh + 1) * LW],
                                        ring_d[:, s, m, a * DH:(a + 1) * DH],
                                        start=(m == 0), stop=(m == KF - 1))
                        if m == KF - 1:
                            ins.then_inc(down_done, 1)

            def h_transposes(c):
                pe.wait_ge(h_ready, c + 1)
                for m in range(KF // HALVES):
                    ins = te.transpose(bank[3][:, m * P:(m + 1) * P], h_r[:, m * P:(m + 1) * P], ident[:])
                ins.then_inc(hT_done, 1)

            pe.wait_ge(table_ready, 2)
            pairs = pair_count(pe)
            odd = pe.value_load(pair_n[0:1, 1:2], min_val=0, max_val=1)
            all_chunks = pe.value_load(chunk_end[0:1, NE - 1:NE], min_val=NE, max_val=MAX_CHUNKS)
            with pe.Fori(0, NE // RING) as it:
                for s in range(RING):
                    e = RING * it + s
                    if s == 0:
                        c0 = pe.value_load(chunk_first[0:1, bass.ds(e, 1)], min_val=0, max_val=MAX_CHUNKS - 1)
                    pe.wait_ge(gu_in[s], 32 * it + 32)
                    gate_up(c0, s)
                    end = pe.value_load(chunk_end[0:1, bass.ds(e, 1)], min_val=1, max_val=MAX_CHUNKS)
                    if s:
                        down_of(c0, s - 1)
                    else:
                        with pe.If(it > 0):
                            down_of(c0, RING - 1)
                    pe.wait_ge(d_in[s], 16 * it + 16)
                    if s == 0:
                        pe.wait_ge(sh_h, 3 * KF + 1)
                    h_transposes(c0)
                    with pe.If(c0 + 1 < end):
                        with pe.Fori(c0 + 1, end) as c:
                            gate_up(c, s)
                            down_of(c, s)
                            h_transposes(c)
                        pe.nop()
                    c0 = end
            with pe.If(odd > 0):
                pe.sem_inc(g_done, HALVES)
                pe.sem_inc(u_done, HALVES)
                down_of(all_chunks, RING - 1)
                pe.sem_inc(hT_done, 1)
                pe.wait_ge(y_ready, all_chunks + FREE1)
                pe.sem_inc(down_done, HALVES)
            with pe.If(odd < 1):
                down_of(2 * pairs, RING - 1)

            shared_up(3 * KF + 1)
            pe.wait_ge(hT_ready, 2 * pairs)
            shared_up(3 * KF + 2)
            shared_up(3 * KF + 3)
            pe.wait_ge(y_ready, 2 * pairs + FREE1)
            shared_down(6)
            shared_down(7)
    return nc


_INS = ["x", "ctx_1024", "mask_1xSxS2_ff0", "L0_xattn_kernel_q", "L0_xattn_bias_q", "L0_xattn_kernel_k",
        "L0_xattn_bias_k", "L0_xattn_kernel_v", "L0_xattn_bias_v", "L0_ffn_gate_w",
        "L0_ffn_shared_gate_w", "L0_ffn_shared_up_w", "L0_ffn_shared_down_w",
        "L0_ffn_routed_gate_w", "L0_ffn_routed_up_w", "L0_ffn_routed_down_w"]


def kernel(**inputs):
    import numpy as _np
    import concourse.bacc as _bacc
    from concourse import mybir as _mybir
    from concourse.bass_utils import run_bass_kernel_spmd as _run

    nc = _bacc.Bacc("TRN2", target_bir_lowering=False, num_devices=1)
    arrays, args = {}, []
    for name in _INS:
        a = _np.ascontiguousarray(inputs[name])
        arrays[f"in_{name}_dram"] = a
        args.append(nc.dram_tensor(f"in_{name}_dram", a.shape, _mybir.dt.from_np(a.dtype), kind="ExternalInput").ap())
    shape = inputs["x"].shape
    args.append(nc.dram_tensor("out_0_dram", shape, _mybir.dt.float32, kind="ExternalOutput").ap())
    build_cross_attention_moe(nc, *args)
    r = _run(nc, [arrays], core_ids=[0])
    return r.results[0]["out_0_dram"]
```
